# Optimizing a Trainium2 kernel written in Bass

```python
import numpy as np
import jax
import jax.numpy as jnp

def _softmax(x, axis=-1):
    return jax.nn.softmax(x, axis=axis)

def _gelu(x):
    return jax.nn.gelu(x, approximate=True)

def _silu(x):
    return jax.nn.silu(x)

def _sigmoid(x):
    return jax.nn.sigmoid(x)

def _layernorm(x, axis=-1, eps=1e-05):
    m = jnp.mean(x, axis=axis, keepdims=True)
    v = jnp.var(x, axis=axis, keepdims=True)
    return (x - m) / jnp.sqrt(v + eps)

def _scatter_add(tgt, idx, src, axis=0):
    return tgt.at[idx].add(src)

def _segment_sum(src, seg, n):
    return jax.ops.segment_sum(src, seg, n)
kernel_name = 'mk_rec_standalone_d1_rec_r8_e1a572'

def setup_inputs(seed: int=0):
    np.random.seed(seed)
    _w = jnp.asarray

    def _rec_inputs():
        import jax
        import jax.numpy as jnp
        _rk = jax.random.key(seed)
        r_last_memory = -0.00493535 + 1.00056 * jax.random.normal(jax.random.fold_in(_rk, 1), (2048, 64), jnp.float32)
        r_all_memory = -0.000612844 + 1.00049 * jax.random.normal(jax.random.fold_in(_rk, 2), (2048, 50, 64), jnp.float32)
        r_seq_item = jnp.stack([jax.random.randint(jax.random.fold_in(jax.random.fold_in(_rk, 3), 0), (2048,), 41, 39933, jnp.int32), jax.random.randint(jax.random.fold_in(jax.random.fold_in(_rk, 3), 1), (2048,), 63, 4989, jnp.int32), jax.random.randint(jax.random.fold_in(jax.random.fold_in(_rk, 3), 2), (2048,), 38, 5000, jnp.int32), jax.random.randint(jax.random.fold_in(jax.random.fold_in(_rk, 3), 3), (2048,), 101, 39979, jnp.int32), jax.random.randint(jax.random.fold_in(jax.random.fold_in(_rk, 3), 4), (2048,), 89, 39994, jnp.int32), jax.random.randint(jax.random.fold_in(jax.random.fold_in(_rk, 3), 5), (2048,), 34, 39958, jnp.int32), jax.random.randint(jax.random.fold_in(jax.random.fold_in(_rk, 3), 6), (2048,), 40, 39975, jnp.int32), jax.random.randint(jax.random.fold_in(jax.random.fold_in(_rk, 3), 7), (2048,), 42, 39988, jnp.int32), jax.random.randint(jax.random.fold_in(jax.random.fold_in(_rk, 3), 8), (2048,), 2, 39974, jnp.int32), jax.random.randint(jax.random.fold_in(jax.random.fold_in(_rk, 3), 9), (2048,), 49, 39949, jnp.int32), jax.random.randint(jax.random.fold_in(jax.random.fold_in(_rk, 3), 10), (2048,), 59, 39959, jnp.int32), jax.random.randint(jax.random.fold_in(jax.random.fold_in(_rk, 3), 11), (2048,), 16, 39997, jnp.int32), jax.random.randint(jax.random.fold_in(jax.random.fold_in(_rk, 3), 12), (2048,), 110, 4987, jnp.int32), jax.random.randint(jax.random.fold_in(jax.random.fold_in(_rk, 3), 13), (2048,), 72, 39966, jnp.int32), jax.random.randint(jax.random.fold_in(jax.random.fold_in(_rk, 3), 14), (2048,), 112, 39977, jnp.int32), jax.random.randint(jax.random.fold_in(jax.random.fold_in(_rk, 3), 15), (2048,), 59, 39987, jnp.int32), jax.random.randint(jax.random.fold_in(jax.random.fold_in(_rk, 3), 16), (2048,), 62, 39918, jnp.int32), jax.random.randint(jax.random.fold_in(jax.random.fold_in(_rk, 3), 17), (2048,), 17, 39863, jnp.int32), jax.random.randint(jax.random.fold_in(jax.random.fold_in(_rk, 3), 18), (2048,), 9, 39975, jnp.int32), jax.random.randint(jax.random.fold_in(jax.random.fold_in(_rk, 3), 19), (2048,), 7, 39923, jnp.int32), jax.random.randint(jax.random.fold_in(jax.random.fold_in(_rk, 3), 20), (2048,), 20, 39948, jnp.int32), jax.random.randint(jax.random.fold_in(jax.random.fold_in(_rk, 3), 21), (2048,), 30, 39988, jnp.int32), jax.random.randint(jax.random.fold_in(jax.random.fold_in(_rk, 3), 22), (2048,), 17, 39972, jnp.int32), jax.random.randint(jax.random.fold_in(jax.random.fold_in(_rk, 3), 23), (2048,), 19, 4997, jnp.int32), jax.random.randint(jax.random.fold_in(jax.random.fold_in(_rk, 3), 24), (2048,), 55, 5000, jnp.int32), jax.random.randint(jax.random.fold_in(jax.random.fold_in(_rk, 3), 25), (2048,), 78, 39998, jnp.int32), jax.random.randint(jax.random.fold_in(jax.random.fold_in(_rk, 3), 26), (2048,), 32, 39967, jnp.int32), jax.random.randint(jax.random.fold_in(jax.random.fold_in(_rk, 3), 27), (2048,), 8, 39993, jnp.int32), jax.random.randint(jax.random.fold_in(jax.random.fold_in(_rk, 3), 28), (2048,), 100, 39935, jnp.int32), jax.random.randint(jax.random.fold_in(jax.random.fold_in(_rk, 3), 29), (2048,), 40, 39939, jnp.int32), jax.random.randint(jax.random.fold_in(jax.random.fold_in(_rk, 3), 30), (2048,), 32, 39969, jnp.int32), jax.random.randint(jax.random.fold_in(jax.random.fold_in(_rk, 3), 31), (2048,), 9, 4999, jnp.int32), jax.random.randint(jax.random.fold_in(jax.random.fold_in(_rk, 3), 32), (2048,), 3, 39989, jnp.int32), jax.random.randint(jax.random.fold_in(jax.random.fold_in(_rk, 3), 33), (2048,), 17, 39997, jnp.int32), jax.random.randint(jax.random.fold_in(jax.random.fold_in(_rk, 3), 34), (2048,), 35, 39953, jnp.int32), jax.random.randint(jax.random.fold_in(jax.random.fold_in(_rk, 3), 35), (2048,), 47, 39995, jnp.int32), jax.random.randint(jax.random.fold_in(jax.random.fold_in(_rk, 3), 36), (2048,), 11, 39967, jnp.int32), jax.random.randint(jax.random.fold_in(jax.random.fold_in(_rk, 3), 37), (2048,), 20, 39918, jnp.int32), jax.random.randint(jax.random.fold_in(jax.random.fold_in(_rk, 3), 38), (2048,), 112, 39986, jnp.int32), jax.random.randint(jax.random.fold_in(jax.random.fold_in(_rk, 3), 39), (2048,), 6, 39937, jnp.int32), jax.random.randint(jax.random.fold_in(jax.random.fold_in(_rk, 3), 40), (2048,), 116, 4996, jnp.int32), jax.random.randint(jax.random.fold_in(jax.random.fold_in(_rk, 3), 41), (2048,), 3, 39965, jnp.int32), jax.random.randint(jax.random.fold_in(jax.random.fold_in(_rk, 3), 42), (2048,), 5, 39958, jnp.int32), jax.random.randint(jax.random.fold_in(jax.random.fold_in(_rk, 3), 43), (2048,), 20, 39979, jnp.int32), jax.random.randint(jax.random.fold_in(jax.random.fold_in(_rk, 3), 44), (2048,), 55, 39988, jnp.int32), jax.random.randint(jax.random.fold_in(jax.random.fold_in(_rk, 3), 45), (2048,), 50, 39974, jnp.int32), jax.random.randint(jax.random.fold_in(jax.random.fold_in(_rk, 3), 46), (2048,), 1, 39990, jnp.int32), jax.random.randint(jax.random.fold_in(jax.random.fold_in(_rk, 3), 47), (2048,), 65, 39994, jnp.int32), jax.random.randint(jax.random.fold_in(jax.random.fold_in(_rk, 3), 48), (2048,), 2, 39934, jnp.int32), jax.random.randint(jax.random.fold_in(jax.random.fold_in(_rk, 3), 49), (2048,), 8, 39935, jnp.int32)], axis=1)
        return (r_last_memory, r_all_memory, r_seq_item)
    r_last_memory, r_all_memory, r_seq_item = _rec_inputs()

    def _L0_rec_setup():
        import jax, jax.numpy as jnp
        import numpy as np
        HIDDEN = 64
        SEQ_LEN = 50
        NUM_ITEM = 5000
        BATCH = 1024
        key = jax.random.key(seed)
        ks = jax.random.split(key, 8)
        all_memory = jax.random.normal(ks[0], (BATCH, SEQ_LEN, HIDDEN), dtype=jnp.float32)
        last_memory = jax.random.normal(ks[1], (BATCH, HIDDEN), dtype=jnp.float32)
        seq_item = jax.random.randint(ks[2], (BATCH, SEQ_LEN), 0, NUM_ITEM)
        s = 1.0 / np.sqrt(HIDDEN)
        Wr = jax.random.normal(ks[3], (HIDDEN, HIDDEN), dtype=jnp.float32) * s
        Ur = jax.random.normal(ks[4], (HIDDEN, HIDDEN), dtype=jnp.float32) * s
        Vr_w = jax.random.normal(ks[5], (HIDDEN,), dtype=jnp.float32) * s
        Vr_b = jnp.zeros((), dtype=jnp.float32)
        return {'all_memory': all_memory, 'last_memory': last_memory, 'seq_item': seq_item, 'Wr': Wr, 'Ur': Ur, 'Vr_w': Vr_w, 'Vr_b': Vr_b}
    _L0_rec_all = _L0_rec_setup()
    _L0_rec_in = {k: v for k, v in _L0_rec_all.items() if k in ('Wr', 'Ur', 'Vr_w', 'Vr_b')}
    del _L0_rec_all
    return {'r_last_memory': r_last_memory, 'r_all_memory': r_all_memory, 'r_seq_item': r_seq_item, 'L0_rec_Wr': _L0_rec_in['Wr'], 'L0_rec_Ur': _L0_rec_in['Ur'], 'L0_rec_Vr_w': _L0_rec_in['Vr_w'], 'L0_rec_Vr_b': _L0_rec_in['Vr_b']}

def reference(r_last_memory, r_all_memory, r_seq_item, L0_rec_Wr, L0_rec_Ur, L0_rec_Vr_w, L0_rec_Vr_b):
    import jax
    import jax.numpy as jnp

    def _L0_rec_ref(all_memory, last_memory, seq_item, Wr, Ur, Vr_w, Vr_b):
        import jax, jax.numpy as jnp
        import numpy as np
        HIDDEN = 64
        SEQ_LEN = 50
        NUM_ITEM = 5000
        BATCH = 1024
        a = jnp.einsum('bsh,kh->bsk', all_memory, Ur)
        l = jnp.einsum('bh,kh->bk', last_memory, Wr)
        h = jnp.tanh(a + l[:, None, :])
        scores = jnp.einsum('bsh,h->bs', h, Vr_w) + Vr_b
        probs = jax.nn.softmax(scores, axis=-1)
        B = probs.shape[0]
        out = jnp.zeros((B, NUM_ITEM), dtype=probs.dtype)
        out = out.at[jnp.arange(B)[:, None], seq_item].add(probs)
        return out
    y = _L0_rec_ref(r_all_memory, r_last_memory, r_seq_item, L0_rec_Wr, L0_rec_Ur, L0_rec_Vr_w, L0_rec_Vr_b)
    return y

_drawn_inputs = setup_inputs


def setup_inputs(seed=0):
    import zlib

    import numpy as np

    out = dict(_drawn_inputs(seed))
    spreads = {}
    factors = {}
    for name, (base, spread) in spreads.items():
        noise = np.random.default_rng([zlib.crc32(name.encode()), seed]).standard_normal(out[name].shape)
        drawn = base * np.exp(spread * noise) if base else spread * noise
        out[name] = jnp.asarray(drawn.astype(out[name].dtype))
    for name, factor in factors.items():
        out[name] = (out[name] * factor).astype(out[name].dtype)
    return out
```

```python
from contextlib import ExitStack

import concourse.bass as bass
from concourse import mybir

F32 = mybir.dt.float32
BF16 = mybir.dt.bfloat16
I32 = mybir.dt.int32
ALU = mybir.AluOpType
ACT = mybir.ActivationFunctionType
AX = mybir.AxisListType

BATCH, SEQ, HID, ITEMS = 2048, 50, 64, 5000
P = 128
PAIR = 2 * SEQ
SUPERS = BATCH // (2 * P)
CHUNKS = PAIR // 2
GROUPS = -(-CHUNKS // 4)

RUN = 130
MAJORS = -(-ITEMS // RUN)
WHOLE = ITEMS // RUN
TAIL = ITEMS - WHOLE * RUN
ROWS = 2 * MAJORS
PARTS = 3

BATCH_PAIRS = 8
SLOTS = P // BATCH_PAIRS
UNITS = (3, 3, 2)
NU = len(UNITS)
AB = 8
STAGES = 4

HEAD = 9
HEAD_SLOT = SLOTS - HEAD
X_PIECES = ((0, 4), (4, 8), (8, GROUPS))
STORES = 3


def chunks_of(g):
    return range(4 * g, min(4 * g + 4, CHUNKS))


def group_at(j, slot, lag):
    at = slot - lag
    if -HEAD <= at < GROUPS - HEAD:
        s, g = j + 1, at + HEAD
    elif at >= HEAD_SLOT:
        s, g = j + 2, at - HEAD_SLOT
    else:
        return None
    if isinstance(j, int) and not 0 <= s < SUPERS:
        return None
    return s, g


def number(s, g):
    return GROUPS * s + g


def freed(s, g):
    return number(s, g) - (1 if g else 0)


def wait(eng, sem, value):
    if not isinstance(value, int) or value > 0:
        eng.wait_ge(sem, value)


def steps(eng, last, body, first=0):
    for j in range(first):
        body(j)
    with eng.Fori(first, last) as j:
        body(j)
    for j in range(last, SUPERS):
        body(j)


def build(nc, last_memory, all_memory, seq_item, Wr, Ur, Vr_w, Vr_b, out):
    x_dram = all_memory.rearrange("(t p r) s h -> t p (r s h)", p=P, r=2)
    last_dram = last_memory.rearrange("(t p r) h -> p t (r h)", p=P, r=2)
    item_dram = seq_item.rearrange("(t p r) s -> p t (r s)", p=P, r=2)
    out_rows = out.rearrange("(t i g r) n -> t i r g n", i=SLOTS, g=BATCH_PAIRS, r=2)

    with ExitStack() as ctx:
        def sb(name, shape, dt=F32):
            return ctx.enter_context(nc.sbuf_tensor(name, shape, dt))

        def bank(name):
            return ctx.enter_context(nc.psum_tensor(name, [P, 512], F32))

        def sem(name):
            return ctx.enter_context(nc.semaphore(name))

        ident = sb("ident", [P, P])
        w_nat = sb("w_nat", [P, 3, P])
        w_t = sb("w_t", [P, 3, P])
        v_col = sb("v_col", [P, 1])
        v_w = sb("v_w", [P, 4, 32])
        vb_col = sb("vb_col", [P, 1])
        iota_a = sb("iota_a", [P, ROWS], BF16)
        iota_b = sb("iota_b", [P, RUN], BF16)
        last_nat = sb("last_nat", [P, SUPERS, P])
        last_t = sb("last_t", [P, SUPERS, P])
        lt = sb("lt", [P, 2, SUPERS, P])
        item = sb("item", [P, SUPERS, PAIR], I32)
        it_f = sb("it_f", [P, SUPERS, PAIR])
        it_neg = sb("it_neg", [P, SUPERS, PAIR])
        it_code = sb("it_code", [P, SUPERS, PAIR])
        it_minor = sb("it_minor", [P, SUPERS, PAIR])
        codes_t = sb("codes_t", [PAIR, SUPERS, 2, P], BF16)
        x = sb("x", [P, PAIR * HID])
        xt = sb("xt", [P, 2, 512])
        z = sb("z", [P, 2, 512])
        h = sb("h", [P, 2, 512])
        s_sb = sb("s_sb", [P, 512])
        sc = sb("sc", [P, PAIR])
        sc_max = sb("sc_max", [P, 2])
        sc_sub = sb("sc_sub", [P, PAIR])
        e = sb("e", [P, PAIR])
        e_sum = sb("e_sum", [P, 2])
        e_inv = sb("e_inv", [P, 2])
        prob = sb("prob", [P, PAIR])
        prob_t = sb("prob_t", [PAIR, P])
        rest1 = sb("rest1", [PAIR, P])
        rest2 = sb("rest2", [PAIR, P])
        ones = sb("ones", [PAIR, P])
        parts = sb("parts", [PAIR, PARTS, P], BF16)
        parts2 = sb("parts2", [PAIR, P, PARTS, 2], BF16)
        codes2 = sb("codes2", [PAIR, 2, P, 2], BF16)
        oh = sb("oh", [PAIR, 2, BATCH_PAIRS, ROWS], BF16)
        a_w = [sb(f"a_w{i}", [PAIR, BATCH_PAIRS, PARTS, ROWS], BF16) for i in range(AB)]
        b_w = [sb(f"b_w{i}", [PAIR, BATCH_PAIRS, RUN], BF16) for i in range(AB)]
        stage = [sb(f"stage{i}", [ROWS, BATCH_PAIRS, RUN]) for i in range(STAGES)]

        xt_ps = bank("xt_ps")
        a_ps = [bank(f"a_ps{i}") for i in range(2)]
        s_ps = bank("s_ps")
        misc_ps = bank("misc_ps")
        out_ps = [bank(f"out_ps{i}") for i in range(NU)]

        zeroed = sem("zeroed")
        consts = sem("consts")
        w_loaded = sem("w_loaded")
        small_loaded = sem("small_loaded")
        last_loaded = sem("last_loaded")
        item_loaded = sem("item_loaded")
        v_ready = sem("v_ready")
        setup_ps = sem("setup_ps")
        setup_sb = sem("setup_sb")
        item_step = sem("item_step")
        codes_ps = sem("codes_ps")
        codes_sb = sem("codes_sb")
        x_loaded = [sem(f"x_loaded{i}") for i in range(len(X_PIECES))]
        xt_full = sem("xt_full")
        xt_ready = sem("xt_ready")
        a_full = sem("a_full")
        z_ready = sem("z_ready")
        h_ready = sem("h_ready")
        h_used = sem("h_used")
        s_ready = sem("s_ready")
        st_full = sem("st_full")
        softmax_step = sem("softmax_step")
        e_ready = sem("e_ready")
        pt_full = sem("pt_full")
        pt_ready = sem("pt_ready")
        part_step = sem("part_step")
        spread = sem("spread")
        oh_ready = sem("oh_ready")
        ab_ready = sem("ab_ready")
        out_full = sem("out_full")
        out_ready = sem("out_ready")
        stored = [sem(f"stored{i}") for i in range(STAGES)]
        block = ctx.enter_context(nc.Block())

        @block.sync
        def _(sp):
            def load_x(s, piece):
                g0, g1 = X_PIECES[piece]
                lo, hi = 4 * g0 * P, min(4 * g1, CHUNKS) * P
                sp.dma_start(x[:, lo:hi], x_dram[s, :, lo:hi]).then_inc(x_loaded[piece], 16)

            def reload_x(s, piece):
                if isinstance(s, int) and s >= SUPERS:
                    return
                sp.wait_ge(xt_full, number(s - 1, X_PIECES[piece][1]))
                load_x(s, piece)

            def body(j, scatter=True):
                for slot in range(SLOTS):
                    if slot == 4:
                        reload_x(j + 2, 2)
                    if scatter:
                        buf = slot % STAGES
                        sp.wait_ge(out_ready, NU + NU * (SLOTS * j + slot + 1))
                        for r in range(2):
                            rows = out_rows[j, slot, r, :, 0:WHOLE * RUN].rearrange("g (m c) -> m g c", c=RUN)
                            sp.dma_start(rows, stage[buf][MAJORS * r:MAJORS * r + WHOLE, :, :])\
                              .then_inc(stored[buf], 16)
                        sp.dma_start(out_rows[j, slot, :, :, WHOLE * RUN:ITEMS],
                                     stage[buf][WHOLE:ROWS:MAJORS, :, 0:TAIL]).then_inc(stored[buf], 16)
                    if slot == HEAD_SLOT + 4:
                        reload_x(j + 3, 0)
                    if slot == HEAD_SLOT + 8:
                        reload_x(j + 3, 1)

            sp.dma_start(last_nat[:, :, :], last_dram).then_inc(last_loaded, 16)
            sp.wait_ge(zeroed, 1)
            for r in range(2):
                half = slice(HID * r, HID * (r + 1))
                sp.dma_start(w_nat[half, 0, half], Ur).then_inc(w_loaded, 16)
                for item_of_block in range(2):
                    sp.dma_start(w_nat[HID * item_of_block:HID * (item_of_block + 1), 1 + r, half], Wr)\
                      .then_inc(w_loaded, 16)
            load_x(0, 0)
            for r in range(2):
                sp.dma_start(v_col[HID * r:HID * (r + 1), :], Vr_w.rearrange("(h a) -> h a", a=1))\
                  .then_inc(small_loaded, 16)
            sp.dma_start(vb_col[:, :], Vr_b.rearrange("(b a) -> b a", a=1).to_broadcast((P, 1)))\
              .then_inc(small_loaded, 16)
            load_x(0, 1)
            sp.dma_start(item[:, :, :], item_dram).then_inc(item_loaded, 16)
            load_x(0, 2)
            reload_x(1, 0)
            reload_x(1, 1)
            body(-1, scatter=False)
            steps(sp, SUPERS - 3, body)
            for buf in range(STAGES):
                sp.wait_ge(stored[buf], 16 * STORES * SUPERS * (SLOTS // STAGES))

        @block.gpsimd
        def _(pool):
            pool.memset(w_nat[:, :, :], 0.0)
            pool.memset(v_w[:, :, :], 0.0).then_inc(zeroed, 1)
            pool.memset(ident[:, :], 0.0).then_inc(consts, 1)
            pool.wait_ge(consts, 1)
            pool.affine_select(out=ident[:, :], in_=ident[:, :], compare_op=ALU.not_equal, fill=1.0, base=0,
                               pattern=[[-1, P]], channel_multiplier=1).then_inc(consts, 1)
            pool.memset(ones[:, :], 1.0)
            pool.iota(iota_a[:, :], pattern=[[1, ROWS]], base=0, channel_multiplier=0,
                      allow_small_or_imprecise_dtypes=True)
            pool.iota(iota_b[:, :], pattern=[[1, RUN]], base=0, channel_multiplier=0,
                      allow_small_or_imprecise_dtypes=True).then_inc(consts, 1)

            def body(j):
                s = j + 1
                if isinstance(s, int) and s >= SUPERS:
                    return
                pool.wait_ge(pt_ready, s + 1)
                wait(pool, spread, 2 * s)
                pool.tensor_tensor(parts[:, 0, :], prob_t[:, :], ones[:, :], ALU.mult).then_inc(part_step, 1)
                pool.wait_ge(part_step, 5 * s + 1)
                pool.tensor_tensor(rest1[:, :], prob_t[:, :], parts[:, 0, :], ALU.subtract).then_inc(part_step, 1)
                pool.wait_ge(part_step, 5 * s + 2)
                pool.tensor_tensor(parts[:, 1, :], rest1[:, :], ones[:, :], ALU.mult).then_inc(part_step, 1)
                pool.wait_ge(part_step, 5 * s + 3)
                pool.tensor_tensor(rest2[:, :], rest1[:, :], parts[:, 1, :], ALU.subtract).then_inc(part_step, 1)
                pool.wait_ge(part_step, 5 * s + 4)
                pool.tensor_tensor(parts[:, 2, :], rest2[:, :], ones[:, :], ALU.mult).then_inc(part_step, 1)

            pool.wait_ge(consts, 3)
            body(-1)
            steps(pool, SUPERS - 1, body)

        @block.scalar
        def _(act):
            act.wait_ge(setup_ps, 1)
            act.activation(w_t[:, :, :], misc_ps[:, 0:3 * P], ACT.Copy).then_inc(setup_sb, 1)
            for half in range(2):
                act.wait_ge(setup_ps, 2 + half)
                act.activation(last_t[:, 4 * half:4 * half + 4, :], a_ps[half][:, :], ACT.Copy).then_inc(setup_sb, 1)
            for k in range(4):
                r, half = k // 2, k % 2
                act.wait_ge(setup_ps, 4 + k)
                act.activation(lt[:, r, 4 * half:4 * half + 4, :], out_ps[k % NU][:, :], ACT.Copy)\
                   .then_inc(setup_sb, 1)

            def body(j, scatter=True, slots=range(SLOTS)):
                s = j + 1
                chain = not isinstance(s, int) or 0 <= s < SUPERS
                for slot in slots:
                    if (at := group_at(j, slot, 0)) is not None:
                        g, n = at[1], len(chunks_of(at[1])) * P
                        act.wait_ge(xt_full, number(*at) + 1)
                        wait(act, a_full, freed(*at))
                        act.activation(xt[:, g % 2, 0:n], xt_ps[:, 0:n], ACT.Copy).then_inc(xt_ready, 1)
                    if chain and slot == 7:
                        act.wait_ge(h_used, number(s, GROUPS))
                        wait(act, st_full, s)
                        act.activation(s_sb[:, :], s_ps[:, :], ACT.Identity, bias=vb_col[:, 0:1]).then_inc(s_ready, 1)
                    if chain and slot == 10:
                        act.wait_ge(softmax_step, 6 * s + 3)
                        act.activation(e[:, :], sc_sub[:, :], ACT.Exp).then_inc(e_ready, 1)
                    if chain and slot == 12:
                        act.wait_ge(pt_full, s + 1)
                        wait(act, part_step, 5 * s)
                        act.activation(prob_t[:, :], misc_ps[0:PAIR, 0:P], ACT.Copy).then_inc(pt_ready, 1)
                    if (at := group_at(j, slot, 2)) is not None:
                        g, n = at[1], len(chunks_of(at[1])) * P
                        act.wait_ge(z_ready, number(*at) + 1)
                        wait(act, h_used, freed(*at))
                        act.activation(h[:, g % 2, 0:n], z[:, g % 2, 0:n], ACT.Tanh).then_inc(h_ready, 1)
                    if scatter:
                        buf, at_pair = slot % STAGES, 0
                        wait(act, stored[buf], 16 * STORES * ((SLOTS // STAGES) * j + slot // STAGES))
                        for u, n in enumerate(UNITS):
                            act.wait_ge(out_full, NU * AB + NU * (SLOTS * j + slot) + u + 1)
                            act.activation(stage[buf][:, at_pair:at_pair + n, :], out_ps[u][0:ROWS, 0:n * RUN],
                                           ACT.Copy).then_inc(out_ready, 1)
                            at_pair += n

            body(-2, scatter=False, slots=range(HEAD_SLOT, SLOTS))
            for t in range(SUPERS):
                act.wait_ge(codes_ps, t + 1)
                act.activation(codes_t[:, t, :, :], out_ps[t % NU][0:PAIR, 0:2 * P], ACT.Copy).then_inc(codes_sb, 1)
            act.sem_inc(out_ready, NU)
            body(-1, scatter=False)
            steps(act, SUPERS - 2, body, first=1)

        @block.vector
        def _(dve):
            def item_math():
                done = [0]

                def link(ins):
                    done[0] += 1
                    ins.then_inc(item_step, 1)
                    return done[0]

                dve.wait_ge(item_loaded, 16)
                link(dve.tensor_copy(it_f[:, :, :], item[:, :, :]))
                yield
                dve.wait_ge(item_step, done[0])
                link(dve.tensor_scalar(it_neg[:, :, :], it_f[:, :, :], 0.0, float(ITEMS), ALU.is_lt, ALU.mult))
                yield
                dve.wait_ge(item_step, done[0])
                link(dve.tensor_tensor(it_f[:, :, :], it_f[:, :, :], it_neg[:, :, :], ALU.add))
                yield
                dve.wait_ge(item_step, done[0])
                link(dve.tensor_scalar(it_f[:, :, :], it_f[:, :, :], -1.0, float(MAJORS * RUN), ALU.max, ALU.min))
                yield
                dve.wait_ge(item_step, done[0])
                link(dve.tensor_scalar(it_neg[:, :, :], it_f[:, :, :], 1.0 / RUN, -(RUN - 1) / (2.0 * RUN),
                                       ALU.mult, ALU.add))
                yield
                dve.wait_ge(item_step, done[0])
                link(dve.tensor_scalar(it_neg[:, :, :], it_neg[:, :, :], ROUND, None, ALU.add))
                yield
                dve.wait_ge(item_step, done[0])
                link(dve.tensor_scalar(it_neg[:, :, :], it_neg[:, :, :], -ROUND, 0.0, ALU.add, ALU.max))
                yield
                dve.wait_ge(item_step, done[0])
                link(dve.tensor_scalar(it_neg[:, :, :], it_neg[:, :, :], float(MAJORS - 1), None, ALU.min))
                yield
                dve.wait_ge(item_step, done[0])
                flat = "p t q -> p (t q)"
                link(dve.scalar_tensor_tensor(it_minor[:, :, :].rearrange(flat), it_neg[:, :, :].rearrange(flat),
                                              -float(RUN), it_f[:, :, :].rearrange(flat), ALU.mult, ALU.add))
                dve.tensor_copy(it_code[:, :, 0:SEQ], it_neg[:, :, 0:SEQ])
                link(dve.tensor_scalar(it_code[:, :, SEQ:PAIR], it_neg[:, :, SEQ:PAIR], float(MAJORS), None,
                                       ALU.add))
                assert done[0] == ITEM_STEPS
                yield

            def add_last(s, g):
                cs = chunks_of(g)
                dve.wait_ge(a_full, number(s, g) + 1)
                wait(dve, h_ready, freed(s, g))
                for r in range(2):
                    own = [c for c in cs if c // (CHUNKS // 2) == r]
                    if not own:
                        continue
                    lo, n = own[0] - cs[0], len(own)
                    view = lambda ap: ap[:, lo * P:(lo + n) * P].rearrange("p (c q) -> p c q", q=P)
                    ins = dve.tensor_tensor(view(z[:, g % 2, :]), view(a_ps[g % 2]),
                                            lt[:, r, s, :].unsqueeze(1).to_broadcast((P, n, P)), ALU.add)
                ins.then_inc(z_ready, 1)

            def softmax_head(s):
                dve.wait_ge(st_full, s + 1)
                wait(dve, softmax_step, 6 * s)
                for t in range(4):
                    for_j = 4 if t < 3 else 1
                    for_c = 4 if t < 3 else 2
                    src = misc_ps[:, :].rearrange("p (c j m) -> p j c m", c=4, j=4)
                    dst = sc[:, 32 * t:32 * t + 8 * for_j if t < 3 else PAIR]
                    ins = dve.tensor_copy(dst.rearrange("p (j c m) -> p j c m", j=for_j, c=for_c),
                                          src[:, 0:for_j, 0:for_c, 2 * t:2 * t + 2])
                ins.then_inc(softmax_step, 1)
                by_row = lambda ap: ap[:, :].rearrange("p (r s) -> p r s", r=2)
                dve.wait_ge(softmax_step, 6 * s + 1)
                dve.tensor_reduce(sc_max[:, :], by_row(sc), AX.X, ALU.max).then_inc(softmax_step, 1)
                dve.wait_ge(softmax_step, 6 * s + 2)
                dve.tensor_tensor(by_row(sc_sub), by_row(sc), sc_max[:, :].unsqueeze(2).to_broadcast((P, 2, SEQ)),
                                  ALU.subtract).then_inc(softmax_step, 1)

            def softmax_tail(s):
                by_row = lambda ap: ap[:, :].rearrange("p (r s) -> p r s", r=2)
                dve.wait_ge(e_ready, s + 1)
                dve.tensor_reduce(e_sum[:, :], by_row(e), AX.X, ALU.add).then_inc(softmax_step, 1)
                dve.wait_ge(softmax_step, 6 * s + 4)
                dve.reciprocal(e_inv[:, :], e_sum[:, :]).then_inc(softmax_step, 1)
                dve.wait_ge(softmax_step, 6 * s + 5)
                wait(dve, pt_full, s)
                dve.tensor_tensor(by_row(prob), by_row(e), e_inv[:, :].unsqueeze(2).to_broadcast((P, 2, SEQ)),
                                  ALU.mult).then_inc(softmax_step, 1)

            def spread_parts(j):
                dve.wait_ge(part_step, 5 * (j + 1))
                wait(dve, ab_ready, SLOTS * j)
                dve.tensor_copy(parts2[:, :, :, :],
                                parts[:, :, :].rearrange("k c q -> k q c").unsqueeze(3)
                                .to_broadcast((PAIR, P, PARTS, 2))).then_inc(spread, 1)
                dve.tensor_copy(codes2[:, :, :, :],
                                codes_t[:, j, :, :].unsqueeze(3).to_broadcast((PAIR, 2, P, 2))).then_inc(spread, 1)
                dve.wait_ge(spread, 2 * (j + 1))

            def make_ab(j, i):
                n = SLOTS * j + i
                pairs = slice(BATCH_PAIRS * i, BATCH_PAIRS * (i + 1))
                kg = (PAIR, BATCH_PAIRS)
                dve.wait_ge(out_full, NU * (n + 1))
                two = "k (m a) -> k m a"
                ia = iota_a[0:PAIR, :].rearrange(two, a=2).unsqueeze(1).to_broadcast((*kg, ROWS // 2, 2))
                code = codes2[:, 0, pairs, :].unsqueeze(2).to_broadcast((*kg, ROWS // 2, 2))
                dve.tensor_tensor(oh[:, i % 2, :, :].rearrange("k g (m a) -> k g m a", a=2), ia, code,
                                  ALU.is_equal).then_inc(oh_ready, 1)
                ib = iota_b[0:PAIR, :].rearrange(two, a=2).unsqueeze(1).to_broadcast((*kg, RUN // 2, 2))
                minor = codes2[:, 1, pairs, :].unsqueeze(2).to_broadcast((*kg, RUN // 2, 2))
                dve.tensor_tensor(b_w[i % AB][:, :, :].rearrange("k g (m a) -> k g m a", a=2), ib, minor,
                                  ALU.is_equal)
                dve.wait_ge(oh_ready, n + 1)
                shape = (*kg, PARTS, ROWS // 2, 2)
                plain = oh[:, i % 2, :, :].rearrange("k g (m a) -> k g m a", a=2).unsqueeze(2).to_broadcast(shape)
                weight = parts2[:, pairs, :, :].unsqueeze(3).to_broadcast(shape)
                dve.tensor_tensor(a_w[i % AB][:, :, :, :].rearrange("k g c (m a) -> k g c m a", a=2), plain, weight,
                                  ALU.mult).then_inc(ab_ready, 1)

            def body(j, scatter=True, slots=range(SLOTS), between=None):
                s = j + 1
                chain = not isinstance(s, int) or 0 <= s < SUPERS
                for slot in slots:
                    if scatter:
                        make_ab(j, slot)
                    if (at := group_at(j, slot, 2)) is not None:
                        add_last(*at)
                    if between is not None:
                        next(between, None)
                    if chain and slot == 9:
                        softmax_head(s)
                    if chain and slot == 11:
                        softmax_tail(s)
                    if chain and slot == SLOTS - 1:
                        spread_parts(s)

            dve.wait_ge(zeroed, 1)
            dve.wait_ge(small_loaded, 48)
            for t in range(4):
                for half in range(2):
                    rows = slice(HID * half, HID * (half + 1))
                    ins = dve.tensor_copy(v_w[rows, t, 2 * t + half:2 * t + half + 1], v_col[rows, 0:1])
            ins.then_inc(v_ready, 1)
            dve.wait_ge(setup_sb, 7)
            math = item_math()
            body(-2, scatter=False, slots=range(HEAD_SLOT, SLOTS), between=math)
            for _ in math:
                pass
            dve.wait_ge(consts, 3)
            dve.wait_ge(codes_sb, SUPERS)
            body(-1, scatter=False)
            steps(dve, SUPERS - 2, body)

        @block.tensor
        def _(pe):
            def transpose(dst, src):
                return pe.transpose(dst, src, ident[0:src.shape[0], 0:src.shape[0]])

            def body(j, scatter=True, slots=range(SLOTS)):
                s = j + 1
                chain = not isinstance(s, int) or 0 <= s < SUPERS
                for slot in slots:
                    if (at := group_at(j, slot, 3)) is not None:
                        g, n = at[1], len(chunks_of(at[1])) * P
                        pe.wait_ge(h_ready, number(*at) + 1)
                        if g == 0:
                            wait(pe, s_ready, at[0])
                        strip = slice(32 * (g % 4), 32 * (g % 4) + 32)
                        pe.matmul(s_ps[strip, 0:n], v_w[:, g // 4, :], h[:, g % 2, 0:n], start=g < 4,
                                  stop=g + 4 >= GROUPS, skip_group_check=True).then_inc(h_used, 1)
                    if (at := group_at(j, slot, 0)) is not None:
                        g = at[1]
                        for piece, (g0, _) in enumerate(X_PIECES):
                            if g == g0:
                                pe.wait_ge(x_loaded[piece], 16 * (at[0] + 1))
                        wait(pe, xt_ready, number(*at))
                        for k, c in enumerate(chunks_of(g)):
                            ins = transpose(xt_ps[:, k * P:(k + 1) * P], x[:, c * P:(c + 1) * P])
                        ins.then_inc(xt_full, 1)
                    if (at := group_at(j, slot, 1)) is not None:
                        g, n = at[1], len(chunks_of(at[1])) * P
                        pe.wait_ge(xt_ready, number(*at) + 1)
                        wait(pe, z_ready, freed(*at))
                        pe.matmul(a_ps[g % 2][:, 0:n], w_t[:, 0, :], xt[:, g % 2, 0:n], start=True, stop=True)\
                          .then_inc(a_full, 1)
                    if scatter:
                        buf, pair = slot % AB, 0
                        pe.wait_ge(ab_ready, SLOTS * j + slot + 1)
                        for u, n in enumerate(UNITS):
                            pe.wait_ge(out_ready, NU * (SLOTS * j + slot) + u + 1)
                            for q in range(n):
                                for part in range(PARTS):
                                    ins = pe.matmul(out_ps[u][0:ROWS, q * RUN:(q + 1) * RUN],
                                                    a_w[buf][:, pair, part, :], b_w[buf][:, pair, :],
                                                    start=part == 0, stop=part == PARTS - 1)
                                pair += 1
                            ins.then_inc(out_full, 1)
                    if chain and slot == 8:
                        pe.wait_ge(s_ready, s + 1)
                        wait(pe, pt_ready, s)
                        for c in range(4):
                            ins = transpose(misc_ps[:, c * P:(c + 1) * P], s_sb[:, c * P:(c + 1) * P])
                        ins.then_inc(st_full, 1)
                    if chain and slot == 11:
                        pe.wait_ge(softmax_step, 6 * s + 6)
                        transpose(misc_ps[0:PAIR, 0:P], prob[:, :]).then_inc(pt_full, 1)

            pe.wait_ge(consts, 2)
            pe.wait_ge(w_loaded, 6 * 16)
            for k in range(3):
                ins = transpose(misc_ps[:, k * P:(k + 1) * P], w_nat[:, k, :])
            ins.then_inc(setup_ps, 1)
            pe.wait_ge(last_loaded, 16)
            for half in range(2):
                for k in range(4):
                    ins = transpose(a_ps[half][:, k * P:(k + 1) * P], last_nat[:, 4 * half + k, :])
                ins.then_inc(setup_ps, 1)
            for k in range(4):
                r, half = k // 2, k % 2
                pe.wait_ge(setup_sb, 2 + half)
                if k >= NU:
                    pe.wait_ge(setup_sb, 4 + k - NU)
                pe.matmul(out_ps[k % NU][:, :], w_t[:, 1 + r, :], last_t[:, 4 * half:4 * half + 4, :],
                          start=True, stop=True).then_inc(setup_ps, 1)
            pe.wait_ge(v_ready, 1)
            pe.sem_inc(out_full, NU * AB)
            body(-2, scatter=False, slots=range(HEAD_SLOT, SLOTS))
            pe.wait_ge(item_step, ITEM_STEPS)
            pe.wait_ge(setup_sb, 7)
            for t in range(SUPERS):
                if t >= NU:
                    pe.wait_ge(codes_sb, t - NU + 1)
                transpose(out_ps[t % NU][0:PAIR, 0:P], it_code[:, t, :])
                transpose(out_ps[t % NU][0:PAIR, P:2 * P], it_minor[:, t, :]).then_inc(codes_ps, 1)
            body(-1, scatter=False)
            pe.wait_ge(codes_sb, SUPERS)
            steps(pe, SUPERS - 2, body)


ROUND = 1.5 * 2.0 ** 23
ITEM_STEPS = 10


def kernel(**inputs):
    import numpy as np
    import concourse.bacc as bacc
    from concourse.bass_utils import run_bass_kernel_spmd

    nc = bacc.Bacc("TRN2", target_bir_lowering=False, num_devices=1)
    names = ["r_last_memory", "r_all_memory", "r_seq_item", "L0_rec_Wr", "L0_rec_Ur", "L0_rec_Vr_w", "L0_rec_Vr_b"]
    arrays, args = {}, []
    for name in names:
        a = np.ascontiguousarray(inputs[name])
        if a.ndim == 0:
            a = a.reshape(1)
        arrays[name] = a
        args.append(nc.dram_tensor(name, a.shape, mybir.dt.from_np(a.dtype), kind="ExternalInput").ap())
    out = nc.dram_tensor("out", (BATCH, ITEMS), F32, kind="ExternalOutput").ap()
    build(nc, *args, out)
    r = run_bass_kernel_spmd(nc, [arrays], core_ids=[0])
    return r.results[0]["out"]
```

```python
from contextlib import ExitStack

import concourse.bass as bass
from concourse import mybir

F32 = mybir.dt.float32
BF16 = mybir.dt.bfloat16
I32 = mybir.dt.int32
ALU = mybir.AluOpType
ACT = mybir.ActivationFunctionType
AX = mybir.AxisListType

BATCH, SEQ, HID, ITEMS = 2048, 50, 64, 5000
P = 128
PAIR = 2 * SEQ
SUPERS = BATCH // (2 * P)
CHUNKS = PAIR // 2
GROUPS = -(-CHUNKS // 4)

RUN = 128
MAJORS = -(-ITEMS // RUN)
WHOLE = ITEMS // RUN
TAIL = ITEMS - WHOLE * RUN
ROWS = 2 * MAJORS
PARTS = 3

BATCH_PAIRS = 8
SLOTS = P // BATCH_PAIRS
UNIT = 4
NU = BATCH_PAIRS // UNIT
OUT_BANKS = 3
PLAIN = 16
LEAD = 12
AB = 4
STAGES = 4

HEAD = 9
HEAD_SLOT = SLOTS - HEAD
KINDS = 5
X_PIECES = ((0, 1), (1, 4), (4, 8), (8, GROUPS))
STORES = 3


def chunks_of(g):
    return range(4 * g, min(4 * g + 4, CHUNKS))


def kind_of(g):
    return g % 2 if g < 6 else 2 if g == 6 else 3 + (g - 7) % 2


def group_at(j, slot, lag):
    at = slot - lag
    if -HEAD <= at < GROUPS - HEAD:
        s, g = j + 1, at + HEAD
    elif at >= HEAD_SLOT:
        s, g = j + 2, at - HEAD_SLOT
    else:
        return None
    if isinstance(j, int) and not 0 <= s < SUPERS:
        return None
    return s, g


def unit_before(i):
    if i >= OUT_BANKS:
        return i - OUT_BANKS
    units = NU * SLOTS
    return max(k for k in range(units) if k % OUT_BANKS == i) - units


def number(s, g):
    return GROUPS * s + g


def freed(s, g):
    return number(s, g) - (1 if g else 0)


def wait(eng, sem, value):
    if not isinstance(value, int) or value > 0:
        eng.wait_ge(sem, value)


def steps(eng, last, body, first=0):
    for j in range(first):
        body(j)
    with eng.Fori(first, last) as j:
        body(j)
    for j in range(last, SUPERS):
        body(j)


def build(nc, last_memory, all_memory, seq_item, Wr, Ur, Vr_w, Vr_b, out):
    x_dram = all_memory.rearrange("(t p r) s h -> t p (r s h)", p=P, r=2)
    last_dram = last_memory.rearrange("(t p r) h -> p t (r h)", p=P, r=2)
    item_dram = seq_item.rearrange("(t p r) s -> p t (r s)", p=P, r=2)
    out_rows = out.rearrange("(t i g r) n -> t i r g n", i=SLOTS, g=BATCH_PAIRS, r=2)

    with ExitStack() as ctx:
        def sb(name, shape, dt=F32):
            return ctx.enter_context(nc.sbuf_tensor(name, shape, dt))

        def bank(name):
            return ctx.enter_context(nc.psum_tensor(name, [P, 512], F32))

        def sem(name):
            return ctx.enter_context(nc.semaphore(name))

        ident = sb("ident", [P, P])
        w_nat = sb("w_nat", [HID, 3, HID])
        w_t = sb("w_t", [P, 2, HID])
        v_col = sb("v_col", [P, 1])
        v_w = sb("v_w", [P, 4, 32])
        vb_col = sb("vb_col", [P, 1])
        iota_a = sb("iota_a", [P, ROWS], BF16)
        iota_b = sb("iota_b", [P, RUN], BF16)
        last_in = sb("last_in", [P, SUPERS, P])
        last_nat = sb("last_nat", [P, SUPERS, 2, 2, HID])
        last_t = sb("last_t", [P, SUPERS, 2, P])
        item = sb("item", [P, SUPERS, PAIR], I32)
        it_f = sb("it_f", [P, SUPERS, PAIR])
        it_neg = sb("it_neg", [P, SUPERS, PAIR])
        it_code = sb("it_code", [P, SUPERS, PAIR])
        it_minor = sb("it_minor", [P, SUPERS, PAIR])
        codes_t = sb("codes_t", [PAIR, SUPERS, 2, P], BF16)
        x = sb("x", [P, PAIR * HID])
        xt = sb("xt", [P, KINDS, 2, 512])
        h = sb("h", [P, 2, 512])
        s_sb = sb("s_sb", [P, 512])
        sc = sb("sc", [P, PAIR])
        sc_max = sb("sc_max", [P, 2])
        sc_sub = sb("sc_sub", [P, PAIR])
        e = sb("e", [P, PAIR])
        e_sum = sb("e_sum", [P, 2])
        e_inv = sb("e_inv", [P, 2])
        prob = sb("prob", [P, PAIR])
        prob_t = sb("prob_t", [PAIR, P])
        rest1 = sb("rest1", [PAIR, P])
        rest2 = sb("rest2", [PAIR, P])
        ones = sb("ones", [PAIR, P])
        parts = sb("parts", [PAIR, PARTS, P], BF16)
        parts2 = sb("parts2", [PAIR, P, PARTS, 2], BF16)
        codes2 = sb("codes2", [PAIR, 2, P, 2], BF16)
        a_w = [sb(f"a_w{i}", [PAIR, BATCH_PAIRS, PARTS, ROWS], BF16) for i in range(AB)]
        oh = [sb(f"oh{i}", [PAIR, BATCH_PAIRS, ROWS], BF16) for i in range(PLAIN)]
        b_w = [sb(f"b_w{i}", [PAIR, BATCH_PAIRS, RUN], BF16) for i in range(PLAIN)]
        stage = [sb(f"stage{i}", [ROWS, BATCH_PAIRS, RUN]) for i in range(STAGES)]

        xt_ps = bank("xt_ps")
        a_ps = [bank(f"a_ps{i}") for i in range(2)]
        s_ps = bank("s_ps")
        misc_ps = bank("misc_ps")
        out_ps = [bank(f"out_ps{i}") for i in range(OUT_BANKS)]
        SETUP_BANKS = [*out_ps, misc_ps]

        zeroed = sem("zeroed")
        consts = sem("consts")
        w_loaded = sem("w_loaded")
        w_twice = sem("w_twice")
        v_loaded = sem("v_loaded")
        vb_loaded = sem("vb_loaded")
        last_loaded = sem("last_loaded")
        rest_loaded = sem("rest_loaded")
        item_loaded = sem("item_loaded")
        last_twice = sem("last_twice")
        v_ready = sem("v_ready")
        setup_ps = sem("setup_ps")
        setup_sb = sem("setup_sb")
        last_rest = sem("last_rest")
        item_step = sem("item_step")
        codes_ps = sem("codes_ps")
        codes_sb = sem("codes_sb")
        x_loaded = [sem(f"x_loaded{i}") for i in range(len(X_PIECES))]
        xt_full = sem("xt_full")
        xt_low = sem("xt_low")
        xt_high = sem("xt_high")
        first_filled = sem("first_filled")
        fill_0 = sem("fill_0")
        fill_1 = sem("fill_1")
        a_full = sem("a_full")
        h_ready = sem("h_ready")
        h_used = sem("h_used")
        s_ready = sem("s_ready")
        st_full = sem("st_full")
        softmax_step = sem("softmax_step")
        e_ready = sem("e_ready")
        pt_full = sem("pt_full")
        pt_ready = sem("pt_ready")
        part_step = sem("part_step")
        spread = sem("spread")
        codes_spread = sem("codes_spread")
        oh_ready = sem("oh_ready")
        ab_ready = sem("ab_ready")
        out_full = sem("out_full")
        out_ready = sem("out_ready")
        stored = [sem(f"stored{i}") for i in range(STAGES)]
        block = ctx.enter_context(nc.Block())

        def first_fill(tile, half, copied):
            part = slice(HID * (1 - half), HID * (2 - half))
            return (xt[part, tile, half, :].rearrange("p (c q) -> p c q", q=P),
                    copied[part, 0:P].unsqueeze(1).to_broadcast((HID, 4, P)))

        @block.sync
        def _(sp):
            def load_x(s, piece):
                g0, g1 = X_PIECES[piece]
                lo, hi = 4 * g0 * P, min(4 * g1, CHUNKS) * P
                sp.dma_start(x[:, lo:hi], x_dram[s, :, lo:hi]).then_inc(x_loaded[piece], 16)

            def reload_x(s, piece):
                if isinstance(s, int) and s >= SUPERS:
                    return
                sp.wait_ge(xt_full, number(s - 1, X_PIECES[piece][1]))
                load_x(s, piece)

            def fill_last(s, row):
                for half in range(2):
                    part = slice(HID * (1 - half), HID * (2 - half))

                    def copy(tile, c0, c1, r, done):
                        dst = xt[part, tile, half, c0 * P:c1 * P].rearrange("p (c q) -> p c q", q=P)
                        src = last_t[part, s, r, :].unsqueeze(1).to_broadcast((HID, c1 - c0, P))
                        sp.dma_start(dst, src).then_inc(done, 16)

                    if row == 0:
                        if not isinstance(s, int) or s > 0:
                            copy(0, 0, 4, 0, fill_0)
                            copy(1, 0, 4, 0, fill_0)
                        copy(2, 0, 1, 0, fill_0)
                        copy(2, 1, 4, 1, fill_0)
                    else:
                        copy(3, 0, 4, 1, fill_1)
                        copy(4, 0, 4, 1, fill_1)

            def refill_last(s, row):
                if isinstance(s, int) and s >= SUPERS:
                    return
                sp.wait_ge(a_full, number(s - 1, GROUPS if row else 7))
                fill_last(s, row)

            def body(j, scatter=True):
                for slot in range(SLOTS):
                    if slot == 4:
                        reload_x(j + 2, 3)
                    if slot == 5:
                        refill_last(j + 2, 1)
                    if scatter:
                        buf = slot % STAGES
                        sp.wait_ge(out_ready, OUT_BANKS + NU * (SLOTS * j + slot + 1))
                        for r in range(2):
                            rows = out_rows[j, slot, r, :, 0:WHOLE * RUN].rearrange("g (m c) -> m g c", c=RUN)
                            sp.dma_start(rows, stage[buf][MAJORS * r:MAJORS * r + WHOLE, :, :])\
                              .then_inc(stored[buf], 16)
                        sp.dma_start(out_rows[j, slot, :, :, WHOLE * RUN:ITEMS],
                                     stage[buf][WHOLE:ROWS:MAJORS, :, 0:TAIL]).then_inc(stored[buf], 16)
                    if slot == HEAD_SLOT + 4:
                        reload_x(j + 3, 0)
                        reload_x(j + 3, 1)
                    if slot == HEAD_SLOT + 8:
                        reload_x(j + 3, 2)
                        refill_last(j + 3, 0)

            for k, w in enumerate((Ur, Wr)):
                sp.dma_start(w_nat[:, k, :], w).then_inc(w_loaded, 16)
            sp.dma_start(last_in[:, 0, :], last_dram[:, 0, :]).then_inc(last_loaded, 16)
            load_x(0, 0)
            load_x(0, 1)
            for r in range(2):
                sp.dma_start(v_col[HID * r:HID * (r + 1), :], Vr_w.rearrange("(h a) -> h a", a=1))\
                  .then_inc(v_loaded, 16)
            sp.dma_start(item[:, :, :], item_dram).then_inc(item_loaded, 16)
            sp.dma_start(last_in[:, 1:SUPERS, :], last_dram[:, 1:SUPERS, :]).then_inc(rest_loaded, 16)
            load_x(0, 2)
            sp.wait_ge(setup_sb, 2)
            fill_last(0, 0)
            fill_last(0, 1)
            sp.dma_start(vb_col[:, :], Vr_b.rearrange("(b a) -> b a", a=1).to_broadcast((P, 1)))\
              .then_inc(vb_loaded, 16)
            load_x(0, 3)
            reload_x(1, 0)
            reload_x(1, 1)
            reload_x(1, 2)
            sp.wait_ge(last_rest, len(SETUP_BANKS))
            refill_last(1, 0)
            body(-1, scatter=False)
            steps(sp, SUPERS - 3, body)
            for buf in range(STAGES):
                sp.wait_ge(stored[buf], 16 * STORES * SUPERS * (SLOTS // STAGES))

        @block.gpsimd
        def _(pool):
            pool.memset(v_w[:, :, :], 0.0).then_inc(zeroed, 1)
            pool.memset(ident[:, :], 0.0).then_inc(consts, 1)
            pool.wait_ge(consts, 1)
            pool.affine_select(out=ident[:, :], in_=ident[:, :], compare_op=ALU.not_equal, fill=1.0, base=0,
                               pattern=[[-1, P]], channel_multiplier=1).then_inc(consts, 1)
            pool.memset(ones[:, :], 1.0)
            pool.iota(iota_a[:, :], pattern=[[1, ROWS]], base=0, channel_multiplier=0,
                      allow_small_or_imprecise_dtypes=True)
            pool.iota(iota_b[:, :], pattern=[[1, RUN]], base=0, channel_multiplier=0,
                      allow_small_or_imprecise_dtypes=True).then_inc(consts, 1)

            def body(j):
                s = j + 1
                if isinstance(s, int) and s >= SUPERS:
                    return
                pool.wait_ge(pt_ready, s + 1)
                wait(pool, spread, s)
                pool.tensor_tensor(parts[:, 0, :], prob_t[:, :], ones[:, :], ALU.mult).then_inc(part_step, 1)
                pool.wait_ge(part_step, 5 * s + 1)
                pool.tensor_tensor(rest1[:, :], prob_t[:, :], parts[:, 0, :], ALU.subtract).then_inc(part_step, 1)
                pool.wait_ge(part_step, 5 * s + 2)
                pool.tensor_tensor(parts[:, 1, :], rest1[:, :], ones[:, :], ALU.mult).then_inc(part_step, 1)
                pool.wait_ge(part_step, 5 * s + 3)
                pool.tensor_tensor(rest2[:, :], rest1[:, :], parts[:, 1, :], ALU.subtract).then_inc(part_step, 1)
                pool.wait_ge(part_step, 5 * s + 4)
                pool.tensor_tensor(parts[:, 2, :], rest2[:, :], ones[:, :], ALU.mult).then_inc(part_step, 1)

            pool.wait_ge(consts, 3)
            body(-1)
            steps(pool, SUPERS - 1, body)

        @block.scalar
        def _(act):
            act.wait_ge(setup_ps, 1)
            act.activation(w_t[:, :, :], misc_ps[:, 0:P], ACT.Copy).then_inc(setup_sb, 1)
            act.wait_ge(setup_ps, 2)
            act.activation(last_t[:, 0, :, :], a_ps[0][:, 0:2 * P], ACT.Copy).then_inc(setup_sb, 1)
            for half in range(2):
                dst, src = first_fill(0, half, a_ps[0])
                act.activation(dst, src, ACT.Copy).then_inc(first_filled, 1)

            def body(j, scatter=True, slots=range(SLOTS)):
                s = j + 1
                chain = not isinstance(s, int) or 0 <= s < SUPERS
                for slot in slots:
                    if not scatter and slot < SUPERS // 2:
                        act.wait_ge(codes_ps, slot + 1)
                        act.activation(codes_t[:, 2 * slot:2 * slot + 2, :, :], out_ps[slot % OUT_BANKS][0:PAIR, :],
                                       ACT.Copy).then_inc(codes_sb, 1)
                    if (at := group_at(j, slot, 2)) is not None:
                        g, n = at[1], len(chunks_of(at[1])) * P
                        act.wait_ge(a_full, number(*at) + 1)
                        wait(act, h_used, freed(*at))
                        act.activation(h[:, g % 2, 0:n], a_ps[g % 2][:, 0:n], ACT.Tanh).then_inc(h_ready, 1)
                    if (at := group_at(j, slot, 0)) is not None:
                        g, n = at[1], len(chunks_of(at[1])) * P
                        act.wait_ge(xt_full, number(*at) + 1)
                        wait(act, a_full, freed(*at))
                        act.activation(xt[0:HID, kind_of(g), 0, 0:n], xt_ps[0:HID, 0:n], ACT.Copy)\
                           .then_inc(xt_low, 1)
                        if scatter:
                            act.activation(xt[HID:P, kind_of(g), 1, 0:n], xt_ps[HID:P, 0:n], ACT.Copy)\
                               .then_inc(xt_high, 1)
                    if chain and slot == 7:
                        act.wait_ge(h_used, number(s, GROUPS))
                        if not scatter:
                            act.wait_ge(vb_loaded, 16)
                        wait(act, st_full, s)
                        act.activation(s_sb[:, :], s_ps[:, :], ACT.Identity, bias=vb_col[:, 0:1]).then_inc(s_ready, 1)
                    if chain and slot == 10:
                        act.wait_ge(softmax_step, 6 * s + 3)
                        act.activation(e[:, :], sc_sub[:, :], ACT.Exp).then_inc(e_ready, 1)
                    if chain and slot == 12:
                        act.wait_ge(pt_full, s + 1)
                        wait(act, part_step, 5 * s)
                        act.activation(prob_t[:, :], misc_ps[0:PAIR, 0:P], ACT.Copy).then_inc(pt_ready, 1)
                    if scatter:
                        buf = slot % STAGES
                        wait(act, stored[buf], 16 * STORES * ((SLOTS // STAGES) * j + slot // STAGES))
                        for u in range(NU):
                            act.wait_ge(out_full, NU * PLAIN + NU * (SLOTS * j + slot) + u + 1)
                            act.activation(stage[buf][:, UNIT * u:UNIT * (u + 1), :],
                                           out_ps[(NU * slot + u) % OUT_BANKS][0:ROWS, 0:UNIT * RUN],
                                           ACT.Copy).then_inc(out_ready, 1)

            body(-2, scatter=False, slots=range(HEAD_SLOT, SLOTS))
            body(-1, scatter=False)
            act.wait_ge(codes_sb, SUPERS // 2)
            act.sem_inc(out_ready, OUT_BANKS)
            steps(act, SUPERS - 2, body, first=1)

        @block.vector
        def _(dve):
            def item_math(k):
                f, t = it_f[:, :, :], it_neg[:, :, :]
                if k == 0:
                    dve.wait_ge(item_loaded, 16)
                    dve.tensor_copy(f, item[:, :, :]).then_inc(item_step, 1)
                    return
                dve.wait_ge(item_step, k)
                if k == 1:
                    ins = dve.tensor_scalar(t, f, 0.0, float(ITEMS), ALU.is_lt, ALU.mult)
                elif k == 2:
                    ins = dve.tensor_tensor(f, f, t, ALU.add)
                elif k == 3:
                    ins = dve.tensor_scalar(f, f, -1.0, float(MAJORS * RUN), ALU.max, ALU.min)
                elif k == 4:
                    ins = dve.tensor_scalar(t, f, 1.0 / RUN, -(RUN - 1) / (2.0 * RUN), ALU.mult, ALU.add)
                elif k == 5:
                    ins = dve.tensor_scalar(t, t, ROUND, None, ALU.add)
                elif k == 6:
                    ins = dve.tensor_scalar(t, t, -ROUND, 0.0, ALU.add, ALU.max)
                elif k == 7:
                    ins = dve.tensor_scalar(t, t, float(MAJORS - 1), None, ALU.min)
                elif k == 8:
                    flat = "p t q -> p (t q)"
                    ins = dve.scalar_tensor_tensor(it_minor[:, :, :].rearrange(flat), t.rearrange(flat), -float(RUN),
                                                   f.rearrange(flat), ALU.mult, ALU.add)
                else:
                    assert k == ITEM_STEPS - 1
                    dve.tensor_copy(it_code[:, :, 0:SEQ], t[:, :, 0:SEQ])
                    ins = dve.tensor_scalar(it_code[:, :, SEQ:PAIR], t[:, :, SEQ:PAIR], float(MAJORS), None, ALU.add)
                ins.then_inc(item_step, 1)

            def softmax_head(s):
                dve.wait_ge(st_full, s + 1)
                wait(dve, softmax_step, 6 * s)
                for t in range(4):
                    for_j = 4 if t < 3 else 1
                    for_c = 4 if t < 3 else 2
                    src = misc_ps[:, :].rearrange("p (c j m) -> p j c m", c=4, j=4)
                    dst = sc[:, 32 * t:32 * t + 8 * for_j if t < 3 else PAIR]
                    ins = dve.tensor_copy(dst.rearrange("p (j c m) -> p j c m", j=for_j, c=for_c),
                                          src[:, 0:for_j, 0:for_c, 2 * t:2 * t + 2])
                ins.then_inc(softmax_step, 1)
                by_row = lambda ap: ap[:, :].rearrange("p (r s) -> p r s", r=2)
                dve.wait_ge(softmax_step, 6 * s + 1)
                dve.tensor_reduce(sc_max[:, :], by_row(sc), AX.X, ALU.max).then_inc(softmax_step, 1)
                dve.wait_ge(softmax_step, 6 * s + 2)
                dve.tensor_tensor(by_row(sc_sub), by_row(sc), sc_max[:, :].unsqueeze(2).to_broadcast((P, 2, SEQ)),
                                  ALU.subtract).then_inc(softmax_step, 1)

            def softmax_tail(s):
                by_row = lambda ap: ap[:, :].rearrange("p (r s) -> p r s", r=2)
                dve.wait_ge(e_ready, s + 1)
                dve.tensor_reduce(e_sum[:, :], by_row(e), AX.X, ALU.add).then_inc(softmax_step, 1)
                dve.wait_ge(softmax_step, 6 * s + 4)
                dve.reciprocal(e_inv[:, :], e_sum[:, :]).then_inc(softmax_step, 1)
                dve.wait_ge(softmax_step, 6 * s + 5)
                wait(dve, pt_full, s)
                dve.tensor_tensor(by_row(prob), by_row(e), e_inv[:, :].unsqueeze(2).to_broadcast((P, 2, SEQ)),
                                  ALU.mult).then_inc(softmax_step, 1)

            def spread_parts(s):
                dve.wait_ge(part_step, 5 * (s + 1))
                wait(dve, ab_ready, SLOTS * s)
                dve.tensor_copy(parts2[:, :, :, :],
                                parts[:, :, :].rearrange("k c q -> k q c").unsqueeze(3)
                                .to_broadcast((PAIR, P, PARTS, 2))).then_inc(spread, 1)
                dve.wait_ge(spread, s + 1)

            def spread_codes(s):
                wait(dve, oh_ready, SLOTS * s)
                dve.tensor_copy(codes2[:, :, :, :],
                                codes_t[:, s, :, :].unsqueeze(3).to_broadcast((PAIR, 2, P, 2)))\
                   .then_inc(codes_spread, 1)
                dve.wait_ge(codes_spread, s + 1)

            def make_plain(s, i):
                n = SLOTS * s + i
                pairs = slice(BATCH_PAIRS * i, BATCH_PAIRS * (i + 1))
                kg = (PAIR, BATCH_PAIRS)
                dve.wait_ge(out_full, NU * (n + 1))
                two = "k (m a) -> k m a"
                ib = iota_b[0:PAIR, :].rearrange(two, a=2).unsqueeze(1).to_broadcast((*kg, RUN // 2, 2))
                minor = codes2[:, 1, pairs, :].unsqueeze(2).to_broadcast((*kg, RUN // 2, 2))
                dve.tensor_tensor(b_w[i % PLAIN][:, :, :].rearrange("k g (m a) -> k g m a", a=2), ib, minor,
                                  ALU.is_equal)
                ia = iota_a[0:PAIR, :].rearrange(two, a=2).unsqueeze(1).to_broadcast((*kg, ROWS // 2, 2))
                code = codes2[:, 0, pairs, :].unsqueeze(2).to_broadcast((*kg, ROWS // 2, 2))
                dve.tensor_tensor(oh[i % PLAIN][:, :, :].rearrange("k g (m a) -> k g m a", a=2), ia, code,
                                  ALU.is_equal).then_inc(oh_ready, 1)

            def make_a(j, i):
                n = SLOTS * j + i
                pairs = slice(BATCH_PAIRS * i, BATCH_PAIRS * (i + 1))
                dve.wait_ge(oh_ready, n + 1)
                dve.wait_ge(out_full, NU * (n + 1 + PLAIN - AB))
                shape = (PAIR, BATCH_PAIRS, PARTS, ROWS // 2, 2)
                plain = oh[i % PLAIN][:, :, :].rearrange("k g (m a) -> k g m a", a=2).unsqueeze(2).to_broadcast(shape)
                weight = parts2[:, pairs, :, :].unsqueeze(3).to_broadcast(shape)
                dve.tensor_tensor(a_w[i % AB][:, :, :, :].rearrange("k g c (m a) -> k g c m a", a=2), plain, weight,
                                  ALU.mult).then_inc(ab_ready, 1)

            def copy_last(k):
                first = 1 + 2 * k
                n = min(2, SUPERS - first)
                dve.wait_ge(setup_ps, 3 + k)
                dve.tensor_copy(last_t[:, first:first + n, :, :],
                                SETUP_BANKS[k][:, 0:2 * n * P].rearrange("p (t r q) -> p t r q", t=n, r=2))\
                   .then_inc(last_rest, 1)

            def last_twice_over(first, last):
                for r in range(2):
                    ins = dve.tensor_copy(last_nat[:, first:last, r, :, :],
                                          last_in[:, first:last, HID * r:HID * (r + 1)].unsqueeze(2)
                                          .to_broadcast((P, last - first, 2, HID)))
                ins.then_inc(last_twice, 1)

            def place_v():
                dve.wait_ge(zeroed, 1)
                dve.wait_ge(v_loaded, 2 * 16)
                for t in range(4):
                    for half in range(2):
                        rows = slice(HID * half, HID * (half + 1))
                        ins = dve.tensor_copy(v_w[rows, t, 2 * t + half:2 * t + half + 1], v_col[rows, 0:1])
                ins.then_inc(v_ready, 1)

            def body(j, scatter=True, slots=range(SLOTS)):
                s = j + 1
                chain = not isinstance(s, int) or 0 <= s < SUPERS
                for slot in slots:
                    if not scatter and (at := group_at(j, slot, 0)) is not None:
                        g, n = at[1], len(chunks_of(at[1])) * P
                        dve.wait_ge(xt_full, number(*at) + 1)
                        wait(dve, a_full, freed(*at))
                        dve.tensor_copy(xt[HID:P, kind_of(g), 1, 0:n], xt_ps[HID:P, 0:n]).then_inc(xt_high, 1)
                    if not scatter and j == -2:
                        if slot == HEAD_SLOT + 1:
                            place_v()
                        if slot == HEAD_SLOT + 2:
                            dve.wait_ge(rest_loaded, 16)
                            last_twice_over(1, SUPERS)
                        if 0 <= slot - HEAD_SLOT - 4 < len(SETUP_BANKS):
                            copy_last(slot - HEAD_SLOT - 4)
                        for k in range(2 * (slot - HEAD_SLOT - 3), 2 * (slot - HEAD_SLOT - 2)):
                            if 0 <= k < ITEM_STEPS:
                                item_math(k)
                    ahead = slot + LEAD
                    if chain and ahead == SLOTS:
                        if not scatter:
                            dve.wait_ge(codes_sb, SUPERS // 2)
                        spread_codes(s)
                    if scatter:
                        make_a(j, slot)
                        if ahead < SLOTS:
                            make_plain(j, ahead)
                    if ahead >= SLOTS and chain:
                        make_plain(s, ahead - SLOTS)
                    if chain and slot == 9:
                        softmax_head(s)
                    if chain and slot == 11:
                        softmax_tail(s)
                    if chain and slot == (SLOTS - 1 if scatter else SLOTS - 3):
                        spread_parts(s)

            dve.wait_ge(w_loaded, 2 * 16)
            dve.tensor_copy(w_nat[:, 2, :], w_nat[:, 0, :]).then_inc(w_twice, 1)
            dve.wait_ge(last_loaded, 16)
            last_twice_over(0, 1)
            dve.wait_ge(setup_sb, 2)
            for half in range(2):
                dst, src = first_fill(1, half, last_t[:, 0, 0, :])
                dve.tensor_copy(dst, src).then_inc(first_filled, 1)
            body(-2, scatter=False, slots=range(HEAD_SLOT, SLOTS))
            dve.wait_ge(consts, 3)
            body(-1, scatter=False)
            steps(dve, SUPERS - 2, body)

        @block.tensor
        def _(pe):
            def transpose(dst, src):
                return pe.transpose(dst, src, ident[0:src.shape[0], 0:src.shape[0]])

            def transpose_last():
                pe.wait_ge(last_twice, 2)
                pe.wait_ge(setup_sb, 1)
                for k, ps in enumerate(SETUP_BANKS):
                    for q in range(2 * min(2, SUPERS - 1 - 2 * k)):
                        ins = transpose(ps[:, q * P:(q + 1) * P], last_nat[:, 1 + 2 * k + q // 2, q % 2, :, :])
                    ins.then_inc(setup_ps, 1)

            def body(j, scatter=True, slots=range(SLOTS)):
                s = j + 1
                chain = not isinstance(s, int) or 0 <= s < SUPERS
                for slot in slots:
                    if not scatter and slot < SUPERS // 2:
                        ps = out_ps[slot % OUT_BANKS]
                        if slot >= OUT_BANKS:
                            pe.wait_ge(codes_sb, slot - OUT_BANKS + 1)
                        for k, codes in enumerate((it_code, it_minor) * 2):
                            ins = transpose(ps[0:PAIR, k * P:(k + 1) * P], codes[:, 2 * slot + k // 2, :])
                        ins.then_inc(codes_ps, 1)
                    if (at := group_at(j, slot, 3)) is not None:
                        g, n = at[1], len(chunks_of(at[1])) * P
                        if not scatter and at == (0, 0):
                            pe.wait_ge(v_ready, 1)
                        pe.wait_ge(h_ready, number(*at) + 1)
                        if g == 0:
                            wait(pe, s_ready, at[0])
                        strip = slice(32 * (g % 4), 32 * (g % 4) + 32)
                        pe.matmul(s_ps[strip, 0:n], v_w[:, g // 4, :], h[:, g % 2, 0:n], start=g < 4,
                                  stop=g + 4 >= GROUPS, skip_group_check=True).then_inc(h_used, 1)
                    if (at := group_at(j, slot, 0)) is not None:
                        g = at[1]
                        for piece, (g0, _) in enumerate(X_PIECES):
                            if g == g0:
                                pe.wait_ge(x_loaded[piece], 16 * (at[0] + 1))
                        wait(pe, xt_low, number(*at))
                        wait(pe, xt_high, number(*at))
                        for k, c in enumerate(chunks_of(g)):
                            ins = transpose(xt_ps[:, k * P:(k + 1) * P], x[:, c * P:(c + 1) * P])
                        ins.then_inc(xt_full, 1)
                    if (at := group_at(j, slot, 1)) is not None:
                        g, n = at[1], len(chunks_of(at[1])) * P
                        if not scatter and at == (0, 0):
                            pe.wait_ge(setup_sb, 2)
                            pe.wait_ge(first_filled, 4)
                        pe.wait_ge(xt_low, number(*at) + 1)
                        pe.wait_ge(xt_high, number(*at) + 1)
                        if kind_of(g) <= 2:
                            if scatter or at[0] > 0 or g == 6:
                                pe.wait_ge(fill_0, 16 * (8 * at[0] + 4))
                        else:
                            pe.wait_ge(fill_1, 16 * 4 * (at[0] + 1))
                        wait(pe, h_ready, freed(*at))
                        for half in range(2):
                            ins = pe.matmul(a_ps[g % 2][HID * half:HID * (half + 1), 0:n], w_t[:, half, :],
                                            xt[:, kind_of(g), half, 0:n], start=True, stop=True)
                        ins.then_inc(a_full, 1)
                    if not scatter and j == -2 and slot == HEAD_SLOT + 3:
                        transpose_last()
                    if scatter:
                        pe.wait_ge(ab_ready, SLOTS * j + slot + 1)
                        for u in range(NU):
                            unit = NU * slot + u
                            pe.wait_ge(out_ready, OUT_BANKS + NU * SLOTS * j + unit_before(unit) + 1)
                            for q in range(UNIT):
                                pair = UNIT * u + q
                                for part in range(PARTS):
                                    ins = pe.matmul(out_ps[unit % OUT_BANKS][0:ROWS, q * RUN:(q + 1) * RUN],
                                                    a_w[slot % AB][:, pair, part, :], b_w[slot % PLAIN][:, pair, :],
                                                    start=part == 0, stop=part == PARTS - 1)
                            ins.then_inc(out_full, 1)
                    if chain and slot == 8:
                        pe.wait_ge(s_ready, s + 1)
                        wait(pe, pt_ready, s)
                        for c in range(4):
                            ins = transpose(misc_ps[:, c * P:(c + 1) * P], s_sb[:, c * P:(c + 1) * P])
                        ins.then_inc(st_full, 1)
                    if chain and slot == 11:
                        pe.wait_ge(softmax_step, 6 * s + 6)
                        transpose(misc_ps[0:PAIR, 0:P], prob[:, :]).then_inc(pt_full, 1)

            pe.wait_ge(consts, 2)
            pe.wait_ge(w_twice, 1)
            for k in range(2):
                ins = transpose(misc_ps[:, k * HID:(k + 1) * HID], w_nat[:, k:k + 2, :])
            ins.then_inc(setup_ps, 1)
            pe.wait_ge(last_twice, 1)
            for r in range(2):
                ins = transpose(a_ps[0][:, r * P:(r + 1) * P], last_nat[:, 0, r, :, :])
            ins.then_inc(setup_ps, 1)
            pe.sem_inc(out_full, NU * PLAIN)
            body(-2, scatter=False, slots=range(HEAD_SLOT, SLOTS))
            pe.wait_ge(item_step, ITEM_STEPS)
            pe.wait_ge(last_rest, len(SETUP_BANKS))
            body(-1, scatter=False)
            pe.wait_ge(codes_sb, SUPERS // 2)
            steps(pe, SUPERS - 2, body)


ROUND = 1.5 * 2.0 ** 23
ITEM_STEPS = 10


def kernel(**inputs):
    import numpy as np
    import concourse.bacc as bacc
    from concourse.bass_utils import run_bass_kernel_spmd

    nc = bacc.Bacc("TRN2", target_bir_lowering=False, num_devices=1)
    names = ["r_last_memory", "r_all_memory", "r_seq_item", "L0_rec_Wr", "L0_rec_Ur", "L0_rec_Vr_w", "L0_rec_Vr_b"]
    arrays, args = {}, []
    for name in names:
        a = np.ascontiguousarray(inputs[name])
        if a.ndim == 0:
            a = a.reshape(1)
        arrays[name] = a
        args.append(nc.dram_tensor(name, a.shape, mybir.dt.from_np(a.dtype), kind="ExternalInput").ap())
    out = nc.dram_tensor("out", (BATCH, ITEMS), F32, kind="ExternalOutput").ap()
    build(nc, *args, out)
    r = run_bass_kernel_spmd(nc, [arrays], core_ids=[0])
    return r.results[0]["out"]
```

```python
from contextlib import ExitStack

from concourse import mybir

F32 = mybir.dt.float32
BF16 = mybir.dt.bfloat16
I32 = mybir.dt.int32
ALU = mybir.AluOpType
ACT = mybir.ActivationFunctionType
AX = mybir.AxisListType

BATCH, SEQ, HID, ITEMS = 2048, 50, 64, 5000
P = 128
PAIR = 2 * SEQ
SUPERS = BATCH // (2 * P)
CHUNKS = PAIR // 2
GROUPS = -(-CHUNKS // 4)

RUN = 128
MAJORS = -(-ITEMS // RUN)
WHOLE = ITEMS // RUN
TAIL = ITEMS - WHOLE * RUN
ROWS = 2 * MAJORS
PARTS = 3

BATCH_PAIRS = 8
SLOTS = P // BATCH_PAIRS
UNIT = 4
NU = BATCH_PAIRS // UNIT
OUT_BANKS = 3
PLAIN = 16
LEAD = 11
AB = 4
STAGES = 4

HEAD = 7
HEAD_SLOT = SLOTS - HEAD
FIRST_LEAD = 6
LAST_LEAD = 6
CODES_SLOT = 1
SCORES_SLOT = GROUPS + 2 - HEAD
KINDS = 5
X_PIECES = ((0, 1), (1, 4), (4, 8), (8, GROUPS))
STORES = 3
STORE_TWO = SLOTS - 3


def chunks_of(g):
    return range(4 * g, min(4 * g + 4, CHUNKS))


def pool_makes_a(j, i):
    return j_is(j, 0, SUPERS - 2, SUPERS - 1) and i % AB == AB - 1 and i < SLOTS - 1


def made_by_pool(j, i):
    if isinstance(j, int):
        return sum(pool_makes_a(*divmod(n, SLOTS)) for n in range(SLOTS * j + i))
    return made_by_pool(1, 0)


def count_a(j, i):
    return SLOTS * j + i - made_by_pool(j, i)


def j_is(j, *values):
    return isinstance(j, int) and j in values


def plain_at(j, slot):
    i = slot + LEAD
    if j_is(j, -2):
        return None
    if j_is(j, -1):
        i = SLOTS + slot - CODES_SLOT - 1
        return i if SLOTS <= i < SLOTS + FIRST_LEAD and i % 2 == 0 else None
    if j_is(j, 0) and FIRST_LEAD + 2 * slot <= i:
        return FIRST_LEAD + 2 * slot
    if j_is(j, SUPERS - 2) and slot == SLOTS - 1:
        return None
    if j_is(j, SUPERS - 1):
        i = slot + LAST_LEAD
        return i if SLOTS - LAST_LEAD <= i < SLOTS and i % 2 == 0 else None
    return i if i % 2 == 0 else None


def softmax_slot(k, scatter):
    return SCORES_SLOT + k - (0 if scatter else 1)


def kind_of(g):
    return g % 2 if g < 6 else 2 if g == 6 else 3 + (g - 7) % 2


def group_at(j, slot, lag):
    at = slot - lag
    if -HEAD <= at < GROUPS - HEAD:
        s, g = j + 1, at + HEAD
    elif at >= HEAD_SLOT:
        s, g = j + 2, at - HEAD_SLOT
    else:
        return None
    if isinstance(j, int) and not 0 <= s < SUPERS:
        return None
    return s, g


def unit_before(i):
    if i >= OUT_BANKS:
        return i - OUT_BANKS
    units = NU * SLOTS
    return max(k for k in range(units) if k % OUT_BANKS == i) - units


def number(s, g):
    return GROUPS * s + g


def freed(s, g):
    return number(s, g) - (1 if g else 0)


def wait(eng, sem, value):
    if not isinstance(value, int) or value > 0:
        eng.wait_ge(sem, value)


def steps(eng, last, body, first=0):
    for j in range(first):
        body(j)
    with eng.Fori(first, last) as j:
        body(j)
    for j in range(last, SUPERS):
        body(j)


def build(nc, last_memory, all_memory, seq_item, Wr, Ur, Vr_w, Vr_b, out):
    x_dram = all_memory.rearrange("(t p r) s h -> t p (r s h)", p=P, r=2)
    last_dram = last_memory.rearrange("(t p r) h -> p t (r h)", p=P, r=2)
    item_dram = seq_item.rearrange("(t p r) s -> p t (r s)", p=P, r=2)
    out_rows = out.rearrange("(t g r) n -> t r g n", g=P, r=2)

    with ExitStack() as ctx:
        def sb(name, shape, dt=F32):
            return ctx.enter_context(nc.sbuf_tensor(name, shape, dt))

        def bank(name):
            return ctx.enter_context(nc.psum_tensor(name, [P, 512], F32))

        def sem(name):
            return ctx.enter_context(nc.semaphore(name))

        ident = sb("ident", [P, P])
        w_nat = sb("w_nat", [HID, 3, HID])
        w_t = sb("w_t", [P, 2, HID])
        v_col = sb("v_col", [P, 1])
        v_w = sb("v_w", [P, 4, 32])
        vb_col = sb("vb_col", [P, 1])
        iota_a = sb("iota_a", [P, ROWS], BF16)
        iota_b = sb("iota_b", [P, RUN], BF16)
        last_in = sb("last_in", [P, SUPERS, P])
        last_nat = sb("last_nat", [P, SUPERS, 2, 2, HID])
        last_t = sb("last_t", [P, SUPERS, 2, P])
        item = sb("item", [P, SUPERS, PAIR], I32)
        it_f = sb("it_f", [P, SUPERS, PAIR])
        it_neg = sb("it_neg", [P, SUPERS, PAIR])
        it_code = sb("it_code", [P, SUPERS, PAIR])
        it_minor = sb("it_minor", [P, SUPERS, PAIR])
        codes2 = sb("codes2", [PAIR, SUPERS, 2, P, 2], BF16)
        x = sb("x", [P, PAIR * HID])
        xt = sb("xt", [P, KINDS, 2, 512])
        h = sb("h", [P, 2, 512])
        s_sb = sb("s_sb", [P, 512])
        sc = sb("sc", [P, PAIR])
        sc_max = sb("sc_max", [P, 2])
        sc_sub = sb("sc_sub", [P, PAIR])
        e = sb("e", [P, PAIR])
        e_sum = sb("e_sum", [P, 2])
        e_inv = sb("e_inv", [P, 2])
        prob = sb("prob", [P, PAIR])
        prob_t = sb("prob_t", [PAIR, P])
        rest1 = sb("rest1", [PAIR, P])
        rest2 = sb("rest2", [PAIR, P])
        ones = sb("ones", [PAIR, P])
        parts = sb("parts", [PAIR, PARTS, P], BF16)
        parts2 = sb("parts2", [PAIR, P, PARTS, 2], BF16)
        a_w = [sb(f"a_w{i}", [PAIR, BATCH_PAIRS, PARTS, ROWS], BF16) for i in range(AB)]
        oh = [sb(f"oh{i}", [PAIR, 2 * BATCH_PAIRS, ROWS], BF16) for i in range(PLAIN // 2)]
        b_w = [sb(f"b_w{i}", [PAIR, 2 * BATCH_PAIRS, RUN], BF16) for i in range(PLAIN // 2)]
        stage = sb("stage", [ROWS, STAGES, BATCH_PAIRS, RUN])

        xt_ps = bank("xt_ps")
        a_ps = [bank(f"a_ps{i}") for i in range(2)]
        s_ps = bank("s_ps")
        misc_ps = bank("misc_ps")
        out_ps = [bank(f"out_ps{i}") for i in range(OUT_BANKS)]
        setup_banks = [*out_ps, misc_ps]

        zeroed = sem("zeroed")
        consts = sem("consts")
        w_loaded = sem("w_loaded")
        w_twice = sem("w_twice")
        v_loaded = sem("v_loaded")
        vb_loaded = sem("vb_loaded")
        last_loaded = sem("last_loaded")
        rest_loaded = sem("rest_loaded")
        item_loaded = sem("item_loaded")
        last_twice = sem("last_twice")
        v_ready = sem("v_ready")
        setup_ps = sem("setup_ps")
        setup_sb = sem("setup_sb")
        last_rest = sem("last_rest")
        item_step = sem("item_step")
        codes_ps = sem("codes_ps")
        codes_sb = sem("codes_sb")
        x_loaded = [sem(f"x_loaded{i}") for i in range(len(X_PIECES))]
        xt_full = sem("xt_full")
        xt_low = sem("xt_low")
        xt_high = sem("xt_high")
        first_filled = sem("first_filled")
        fill_0 = sem("fill_0")
        fill_1 = sem("fill_1")
        a_full = sem("a_full")
        h_ready = sem("h_ready")
        h_used = sem("h_used")
        s_ready = sem("s_ready")
        st_full = sem("st_full")
        softmax_step = sem("softmax_step")
        e_ready = sem("e_ready")
        pt_full = sem("pt_full")
        pt_ready = sem("pt_ready")
        part_step = sem("part_step")
        spread = sem("spread")
        oh_ready = sem("oh_ready")
        ab_ready = sem("ab_ready")
        a_by_pool = sem("a_by_pool")
        out_full = sem("out_full")
        out_ready = sem("out_ready")
        stored = [sem(f"stored{i}") for i in range(STAGES)]
        block = ctx.enter_context(nc.Block())

        def make_a(eng, j, i, done):
            n = SLOTS * j + i
            pairs = slice(BATCH_PAIRS * i, BATCH_PAIRS * (i + 1))
            half = slice(BATCH_PAIRS * (i % 2), BATCH_PAIRS * (i % 2 + 1))
            eng.wait_ge(oh_ready, n + 1)
            eng.wait_ge(out_full, NU * (n + 1 + PLAIN - AB))
            shape = (PAIR, BATCH_PAIRS, PARTS, ROWS // 2, 2)
            plain = oh[i % PLAIN // 2][:, half, :].rearrange("k g (m a) -> k g m a", a=2).unsqueeze(2)\
                .to_broadcast(shape)
            weight = parts2[:, pairs, :, :].unsqueeze(3).to_broadcast(shape)
            eng.tensor_tensor(a_w[i % AB][:, :, :, :].rearrange("k g c (m a) -> k g c m a", a=2), plain, weight,
                              ALU.mult).then_inc(done, 1)

        def first_fill(tile, half, copied):
            part = slice(HID * (1 - half), HID * (2 - half))
            return (xt[part, tile, half, :].rearrange("p (c q) -> p c q", q=P),
                    copied[part, 0:P].unsqueeze(1).to_broadcast((HID, 4, P)))

        @block.sync
        def _(sp):
            def load_x(s, piece):
                g0, g1 = X_PIECES[piece]
                lo, hi = 4 * g0 * P, min(4 * g1, CHUNKS) * P
                sp.dma_start(x[:, lo:hi], x_dram[s, :, lo:hi]).then_inc(x_loaded[piece], 16)

            def reload_x(s, piece):
                if isinstance(s, int) and s >= SUPERS:
                    return
                sp.wait_ge(xt_full, number(s - 1, X_PIECES[piece][1]))
                load_x(s, piece)

            def fill_last(s, row):
                for half in range(2):
                    part = slice(HID * (1 - half), HID * (2 - half))

                    def copy(tile, c0, c1, r, done):
                        dst = xt[part, tile, half, c0 * P:c1 * P].rearrange("p (c q) -> p c q", q=P)
                        src = last_t[part, s, r, :].unsqueeze(1).to_broadcast((HID, c1 - c0, P))
                        sp.dma_start(dst, src).then_inc(done, 16)

                    if row == 0:
                        if not isinstance(s, int) or s > 0:
                            copy(0, 0, 4, 0, fill_0)
                            copy(1, 0, 4, 0, fill_0)
                        copy(2, 0, 1, 0, fill_0)
                        copy(2, 1, 4, 1, fill_0)
                    else:
                        copy(3, 0, 4, 1, fill_1)
                        copy(4, 0, 4, 1, fill_1)

            def refill_last(s, row):
                if isinstance(s, int) and s >= SUPERS:
                    return
                sp.wait_ge(a_full, number(s - 1, GROUPS if row else 7))
                if isinstance(s, int) and s == 1:
                    sp.wait_ge(last_rest, len(setup_banks))
                fill_last(s, row)

            def store(j, i, n):
                last = i % STAGES
                bufs, pairs = slice(last + 1 - n, last + 1), slice(BATCH_PAIRS * (i + 1 - n), BATCH_PAIRS * (i + 1))
                sp.wait_ge(out_ready, OUT_BANKS + NU * (SLOTS * j + i + 1))
                for r in range(2):
                    sp.dma_start(out_rows[j, r, pairs, 0:WHOLE * RUN].rearrange("g (m c) -> m g c", c=RUN),
                                 stage[MAJORS * r:MAJORS * r + WHOLE, bufs, :, :].rearrange("m b g c -> m (b g) c"))\
                      .then_inc(stored[last], 16)
                sp.dma_start(out_rows[j, :, pairs, WHOLE * RUN:ITEMS],
                             stage[WHOLE:ROWS:MAJORS, bufs, :, 0:TAIL].rearrange("r b g c -> r (b g) c"))\
                  .then_inc(stored[last], 16)

            def body(j, scatter=True, slots=range(SLOTS)):
                for slot in slots:
                    for at, s in ((slot, j + 2), (slot - SLOTS, j + 3)):
                        for piece, (_, end) in enumerate(X_PIECES):
                            if at == end - HEAD:
                                reload_x(s, piece)
                        if at == 8 - HEAD:
                            refill_last(s, 0)
                        if at == GROUPS + 1 - HEAD:
                            refill_last(s, 1)
                    if scatter and not (j_is(j, SUPERS - 1) and slot == STORE_TWO - 1):
                        store(j, slot, 2 if j_is(j, SUPERS - 1) and slot == STORE_TWO else 1)

            for k, w in enumerate((Ur, Wr)):
                sp.dma_start(w_nat[:, k, :], w).then_inc(w_loaded, 16)
            sp.dma_start(last_in[:, 0, :], last_dram[:, 0, :]).then_inc(last_loaded, 16)
            load_x(0, 0)
            load_x(0, 1)
            for r in range(2):
                sp.dma_start(v_col[HID * r:HID * (r + 1), :], Vr_w.rearrange("(h a) -> h a", a=1))\
                  .then_inc(v_loaded, 16)
            sp.dma_start(item[:, :, :], item_dram).then_inc(item_loaded, 16)
            sp.dma_start(last_in[:, 1:SUPERS, :], last_dram[:, 1:SUPERS, :]).then_inc(rest_loaded, 16)
            load_x(0, 2)
            sp.wait_ge(setup_sb, 2)
            fill_last(0, 0)
            fill_last(0, 1)
            sp.dma_start(vb_col[:, :], Vr_b.rearrange("(b a) -> b a", a=1).to_broadcast((P, 1)))\
              .then_inc(vb_loaded, 16)
            load_x(0, 3)
            body(-2, scatter=False, slots=range(HEAD_SLOT, SLOTS))
            body(-1, scatter=False)
            steps(sp, SUPERS - 3, body)
            for buf in range(STAGES):
                less = 1 if buf == (STORE_TWO - 1) % STAGES else 0
                sp.wait_ge(stored[buf], 16 * STORES * (SUPERS * (SLOTS // STAGES) - less))

        @block.gpsimd
        def _(pool):
            pool.memset(v_w[:, :, :], 0.0).then_inc(zeroed, 1)
            pool.memset(ident[:, :], 0.0).then_inc(consts, 1)
            pool.wait_ge(consts, 1)
            pool.affine_select(out=ident[:, :], in_=ident[:, :], compare_op=ALU.not_equal, fill=1.0, base=0,
                               pattern=[[-1, P]], channel_multiplier=1).then_inc(consts, 1)
            pool.memset(ones[:, :], 1.0)
            pool.iota(iota_a[:, :], pattern=[[1, ROWS]], base=0, channel_multiplier=0,
                      allow_small_or_imprecise_dtypes=True)
            pool.iota(iota_b[:, :], pattern=[[1, RUN]], base=0, channel_multiplier=0,
                      allow_small_or_imprecise_dtypes=True).then_inc(consts, 1)

            def body(j):
                s = j + 1
                if isinstance(s, int) and s >= SUPERS:
                    return
                pool.wait_ge(pt_ready, s + 1)
                wait(pool, spread, s)
                pool.tensor_tensor(parts[:, 0, :], prob_t[:, :], ones[:, :], ALU.mult).then_inc(part_step, 1)
                pool.wait_ge(part_step, 5 * s + 1)
                pool.tensor_tensor(rest1[:, :], prob_t[:, :], parts[:, 0, :], ALU.subtract).then_inc(part_step, 1)
                pool.wait_ge(part_step, 5 * s + 2)
                pool.tensor_tensor(parts[:, 1, :], rest1[:, :], ones[:, :], ALU.mult).then_inc(part_step, 1)
                pool.wait_ge(part_step, 5 * s + 3)
                pool.tensor_tensor(rest2[:, :], rest1[:, :], parts[:, 1, :], ALU.subtract).then_inc(part_step, 1)
                pool.wait_ge(part_step, 5 * s + 4)
                pool.tensor_tensor(parts[:, 2, :], rest2[:, :], ones[:, :], ALU.mult).then_inc(part_step, 1)

            def body_and_a(j):
                pool.wait_ge(spread, j + 1)
                for i in range(SLOTS):
                    if i == SLOTS - AB:
                        body(j)
                    if pool_makes_a(j, i):
                        make_a(pool, j, i, a_by_pool)

            pool.wait_ge(consts, 3)
            body(-1)
            body_and_a(0)
            with pool.Fori(1, SUPERS - 2) as j:
                body(j)
            for j in range(SUPERS - 2, SUPERS):
                body_and_a(j)

        @block.scalar
        def _(act):
            act.wait_ge(setup_ps, 1)
            act.activation(w_t[:, :, :], misc_ps[:, 0:P], ACT.Copy).then_inc(setup_sb, 1)
            act.wait_ge(setup_ps, 2)
            act.activation(last_t[:, 0, :, :], a_ps[0][:, 0:2 * P], ACT.Copy).then_inc(setup_sb, 1)
            for half in range(2):
                dst, src = first_fill(0, half, a_ps[0])
                act.activation(dst, src, ACT.Copy).then_inc(first_filled, 1)

            def copy_last(k):
                first = 1 + 2 * k
                n = min(2, SUPERS - first)
                act.wait_ge(setup_ps, 3 + k)
                act.activation(last_t[:, first:first + n, :, :], setup_banks[k][:, 0:2 * n * P], ACT.Copy)\
                   .then_inc(last_rest, 1)

            def body(j, scatter=True, slots=range(SLOTS)):
                s = j + 1
                chain = not isinstance(s, int) or 0 <= s < SUPERS
                for slot in slots:
                    if not scatter and 0 <= (k := slot - CODES_SLOT) < SUPERS // 2:
                        act.wait_ge(codes_ps, k + 1)
                        act.activation(codes2[:, 2 * k:2 * k + 2, :, :, :].rearrange("k t c q a -> k (t c q) a"),
                                       out_ps[k % OUT_BANKS][0:PAIR, :].unsqueeze(2).to_broadcast((PAIR, 4 * P, 2)),
                                       ACT.Copy).then_inc(codes_sb, 1)
                    if (at := group_at(j, slot, 2)) is not None:
                        g, n = at[1], len(chunks_of(at[1])) * P
                        act.wait_ge(a_full, number(*at) + 1)
                        wait(act, h_used, freed(*at))
                        act.activation(h[:, g % 2, 0:n], a_ps[g % 2][:, 0:n], ACT.Tanh).then_inc(h_ready, 1)
                    if (at := group_at(j, slot, 0)) is not None:
                        g, n = at[1], len(chunks_of(at[1])) * P
                        act.wait_ge(xt_full, number(*at) + 1)
                        wait(act, a_full, freed(*at))
                        act.activation(xt[0:HID, kind_of(g), 0, 0:n], xt_ps[0:HID, 0:n], ACT.Copy)\
                           .then_inc(xt_low, 1)
                        if scatter:
                            act.activation(xt[HID:P, kind_of(g), 1, 0:n], xt_ps[HID:P, 0:n], ACT.Copy)\
                               .then_inc(xt_high, 1)
                    if j_is(j, -2) and 0 <= slot - HEAD_SLOT - 3 < len(setup_banks):
                        copy_last(slot - HEAD_SLOT - 3)
                    if chain and slot == SCORES_SLOT:
                        act.wait_ge(h_used, number(s, GROUPS))
                        if not scatter:
                            act.wait_ge(vb_loaded, 16)
                        wait(act, st_full, s)
                        act.activation(s_sb[:, :], s_ps[:, :], ACT.Identity, bias=vb_col[:, 0:1]).then_inc(s_ready, 1)
                    if chain and slot == softmax_slot(2, scatter):
                        act.wait_ge(softmax_step, 6 * s + 3)
                        act.activation(e[:, :], sc_sub[:, :], ACT.Exp).then_inc(e_ready, 1)
                    if chain and slot == softmax_slot(3, scatter):
                        act.wait_ge(pt_full, s + 1)
                        wait(act, part_step, 5 * s)
                        act.activation(prob_t[:, :], misc_ps[0:PAIR, 0:P], ACT.Copy).then_inc(pt_ready, 1)
                    if scatter:
                        buf = slot % STAGES
                        wait(act, stored[buf], 16 * STORES * ((SLOTS // STAGES) * j + slot // STAGES))
                        for u in range(NU):
                            act.wait_ge(out_full, NU * PLAIN + NU * (SLOTS * j + slot) + u + 1)
                            act.activation(stage[:, buf, UNIT * u:UNIT * (u + 1), :],
                                           out_ps[(NU * slot + u) % OUT_BANKS][0:ROWS, 0:UNIT * RUN],
                                           ACT.Copy).then_inc(out_ready, 1)

            body(-2, scatter=False, slots=range(HEAD_SLOT, SLOTS))
            body(-1, scatter=False)
            act.wait_ge(codes_sb, SUPERS // 2)
            act.sem_inc(out_ready, OUT_BANKS)
            steps(act, SUPERS - 2, body, first=1)

        @block.vector
        def _(dve):
            def item_math(k):
                f, t = it_f[:, :, :], it_neg[:, :, :]
                if k == 0:
                    dve.wait_ge(item_loaded, 16)
                    dve.tensor_copy(f, item[:, :, :]).then_inc(item_step, 1)
                    return
                dve.wait_ge(item_step, k)
                if k == 1:
                    ins = dve.tensor_scalar(t, f, 0.0, float(ITEMS), ALU.is_lt, ALU.mult)
                elif k == 2:
                    ins = dve.tensor_tensor(f, f, t, ALU.add)
                elif k == 3:
                    ins = dve.tensor_scalar(f, f, -1.0, float(MAJORS * RUN), ALU.max, ALU.min)
                elif k == 4:
                    ins = dve.tensor_scalar(t, f, 1.0 / RUN, -(RUN - 1) / (2.0 * RUN), ALU.mult, ALU.add)
                elif k == 5:
                    ins = dve.tensor_scalar(t, t, ROUND, None, ALU.add)
                elif k == 6:
                    ins = dve.tensor_scalar(t, t, -ROUND, 0.0, ALU.add, ALU.max)
                elif k == 7:
                    ins = dve.tensor_scalar(t, t, float(MAJORS - 1), None, ALU.min)
                elif k == 8:
                    flat = "p t q -> p (t q)"
                    ins = dve.scalar_tensor_tensor(it_minor[:, :, :].rearrange(flat), t.rearrange(flat), -float(RUN),
                                                   f.rearrange(flat), ALU.mult, ALU.add)
                else:
                    assert k == ITEM_STEPS - 1
                    dve.tensor_copy(it_code[:, :, 0:SEQ], t[:, :, 0:SEQ])
                    ins = dve.tensor_scalar(it_code[:, :, SEQ:PAIR], t[:, :, SEQ:PAIR], float(MAJORS), None, ALU.add)
                ins.then_inc(item_step, 1)

            def softmax_head(s):
                dve.wait_ge(st_full, s + 1)
                wait(dve, softmax_step, 6 * s)
                for t in range(4):
                    for_j = 4 if t < 3 else 1
                    for_c = 4 if t < 3 else 2
                    src = misc_ps[:, :].rearrange("p (c j m) -> p j c m", c=4, j=4)
                    dst = sc[:, 32 * t:32 * t + 8 * for_j if t < 3 else PAIR]
                    ins = dve.tensor_copy(dst.rearrange("p (j c m) -> p j c m", j=for_j, c=for_c),
                                          src[:, 0:for_j, 0:for_c, 2 * t:2 * t + 2])
                ins.then_inc(softmax_step, 1)
                by_row = lambda ap: ap[:, :].rearrange("p (r s) -> p r s", r=2)
                dve.wait_ge(softmax_step, 6 * s + 1)
                dve.tensor_reduce(sc_max[:, :], by_row(sc), AX.X, ALU.max).then_inc(softmax_step, 1)
                dve.wait_ge(softmax_step, 6 * s + 2)
                dve.tensor_tensor(by_row(sc_sub), by_row(sc), sc_max[:, :].unsqueeze(2).to_broadcast((P, 2, SEQ)),
                                  ALU.subtract).then_inc(softmax_step, 1)

            def softmax_tail(s):
                by_row = lambda ap: ap[:, :].rearrange("p (r s) -> p r s", r=2)
                dve.wait_ge(e_ready, s + 1)
                dve.tensor_reduce(e_sum[:, :], by_row(e), AX.X, ALU.add).then_inc(softmax_step, 1)
                dve.wait_ge(softmax_step, 6 * s + 4)
                dve.reciprocal(e_inv[:, :], e_sum[:, :]).then_inc(softmax_step, 1)
                dve.wait_ge(softmax_step, 6 * s + 5)
                wait(dve, pt_full, s)
                dve.tensor_tensor(by_row(prob), by_row(e), e_inv[:, :].unsqueeze(2).to_broadcast((P, 2, SEQ)),
                                  ALU.mult).then_inc(softmax_step, 1)

            def spread_parts(s):
                dve.wait_ge(part_step, 5 * (s + 1))
                wait(dve, ab_ready, count_a(s, 0))
                if isinstance(s, int) and s > 0 and made_by_pool(s, 0) > made_by_pool(s - 1, 0):
                    dve.wait_ge(a_by_pool, made_by_pool(s, 0))
                dve.tensor_copy(parts2[:, :, :, :],
                                parts[:, :, :].rearrange("k c q -> k q c").unsqueeze(3)
                                .to_broadcast((PAIR, P, PARTS, 2))).then_inc(spread, 1)
                dve.wait_ge(spread, s + 1)

            def make_plain(s, i):
                n = SLOTS * s + i
                pairs = slice(BATCH_PAIRS * i, BATCH_PAIRS * (i + 2))
                kg = (PAIR, 2 * BATCH_PAIRS)
                dve.wait_ge(out_full, NU * (n + 2))
                two = "k (m a) -> k m a"
                ib = iota_b[0:PAIR, :].rearrange(two, a=2).unsqueeze(1).to_broadcast((*kg, RUN // 2, 2))
                minor = codes2[:, s, 1, pairs, :].unsqueeze(2).to_broadcast((*kg, RUN // 2, 2))
                dve.tensor_tensor(b_w[i % PLAIN // 2][:, :, :].rearrange("k g (m a) -> k g m a", a=2), ib, minor,
                                  ALU.is_equal)
                ia = iota_a[0:PAIR, :].rearrange(two, a=2).unsqueeze(1).to_broadcast((*kg, ROWS // 2, 2))
                code = codes2[:, s, 0, pairs, :].unsqueeze(2).to_broadcast((*kg, ROWS // 2, 2))
                dve.tensor_tensor(oh[i % PLAIN // 2][:, :, :].rearrange("k g (m a) -> k g m a", a=2), ia, code,
                                  ALU.is_equal).then_inc(oh_ready, 2)

            def last_twice_over(first, last):
                for r in range(2):
                    ins = dve.tensor_copy(last_nat[:, first:last, r, :, :],
                                          last_in[:, first:last, HID * r:HID * (r + 1)].unsqueeze(2)
                                          .to_broadcast((P, last - first, 2, HID)))
                ins.then_inc(last_twice, 1)

            def place_v():
                dve.wait_ge(zeroed, 1)
                dve.wait_ge(v_loaded, 2 * 16)
                for t in range(4):
                    for half in range(2):
                        rows = slice(HID * half, HID * (half + 1))
                        ins = dve.tensor_copy(v_w[rows, t, 2 * t + half:2 * t + half + 1], v_col[rows, 0:1])
                ins.then_inc(v_ready, 1)

            def body(j, scatter=True, slots=range(SLOTS)):
                s = j + 1
                chain = not isinstance(s, int) or 0 <= s < SUPERS
                for slot in slots:
                    if not scatter and (at := group_at(j, slot, 0)) is not None:
                        g, n = at[1], len(chunks_of(at[1])) * P
                        dve.wait_ge(xt_full, number(*at) + 1)
                        wait(dve, a_full, freed(*at))
                        dve.tensor_copy(xt[HID:P, kind_of(g), 1, 0:n], xt_ps[HID:P, 0:n]).then_inc(xt_high, 1)
                    if j_is(j, -2):
                        if slot == HEAD_SLOT + 1:
                            place_v()
                        if slot == HEAD_SLOT + 2:
                            dve.wait_ge(rest_loaded, 16)
                            last_twice_over(1, SUPERS)
                        for k in range(2 * (slot - HEAD_SLOT - 2), 2 * (slot - HEAD_SLOT - 1)):
                            if 0 <= k < ITEM_STEPS:
                                item_math(k)
                    if scatter and not pool_makes_a(j, slot):
                        make_a(dve, j, slot, ab_ready)
                    if j_is(j, -1) and slot == CODES_SLOT + 1:
                        dve.wait_ge(codes_sb, 1)
                    i = plain_at(j, slot)
                    if i is not None and i < SLOTS:
                        make_plain(j, i)
                    elif i is not None and chain:
                        make_plain(s, i - SLOTS)
                    if chain and slot == softmax_slot(2, scatter):
                        softmax_head(s)
                    if chain and slot == softmax_slot(3, scatter):
                        softmax_tail(s)
                    if chain and slot == (SLOTS - 1 if scatter else min(SLOTS - 1, SCORES_SLOT + 5)):
                        spread_parts(s)

            dve.wait_ge(w_loaded, 2 * 16)
            dve.tensor_copy(w_nat[:, 2, :], w_nat[:, 0, :]).then_inc(w_twice, 1)
            dve.wait_ge(last_loaded, 16)
            last_twice_over(0, 1)
            dve.wait_ge(setup_sb, 2)
            for half in range(2):
                dst, src = first_fill(1, half, last_t[:, 0, 0, :])
                dve.tensor_copy(dst, src).then_inc(first_filled, 1)
            body(-2, scatter=False, slots=range(HEAD_SLOT, SLOTS))
            dve.wait_ge(consts, 3)
            body(-1, scatter=False)
            dve.wait_ge(codes_sb, SUPERS // 2)
            steps(dve, SUPERS - 2, body, first=1)

        @block.tensor
        def _(pe):
            def transpose(dst, src):
                return pe.transpose(dst, src, ident[0:src.shape[0], 0:src.shape[0]])

            def transpose_last():
                pe.wait_ge(last_twice, 2)
                pe.wait_ge(setup_sb, 1)
                for k, ps in enumerate(setup_banks):
                    for q in range(2 * min(2, SUPERS - 1 - 2 * k)):
                        ins = transpose(ps[:, q * P:(q + 1) * P], last_nat[:, 1 + 2 * k + q // 2, q % 2, :, :])
                    ins.then_inc(setup_ps, 1)

            def body(j, scatter=True, slots=range(SLOTS)):
                s = j + 1
                chain = not isinstance(s, int) or 0 <= s < SUPERS
                for slot in slots:
                    if not scatter and 0 <= (n := slot - CODES_SLOT) < SUPERS // 2:
                        ps = out_ps[n % OUT_BANKS]
                        pe.wait_ge(item_step, ITEM_STEPS)
                        pe.wait_ge(last_rest, len(setup_banks))
                        if n >= OUT_BANKS:
                            pe.wait_ge(codes_sb, n - OUT_BANKS + 1)
                        for k, codes in enumerate((it_code, it_minor) * 2):
                            ins = transpose(ps[0:PAIR, k * P:(k + 1) * P], codes[:, 2 * n + k // 2, :])
                        ins.then_inc(codes_ps, 1)
                    if (at := group_at(j, slot, 3)) is not None:
                        g, n = at[1], len(chunks_of(at[1])) * P
                        if not scatter and at == (0, 0):
                            pe.wait_ge(v_ready, 1)
                        pe.wait_ge(h_ready, number(*at) + 1)
                        if g == 0:
                            wait(pe, s_ready, at[0])
                        strip = slice(32 * (g % 4), 32 * (g % 4) + 32)
                        pe.matmul(s_ps[strip, 0:n], v_w[:, g // 4, :], h[:, g % 2, 0:n], start=g < 4,
                                  stop=g + 4 >= GROUPS, skip_group_check=True).then_inc(h_used, 1)
                    if (at := group_at(j, slot, 0)) is not None:
                        g = at[1]
                        for piece, (g0, _) in enumerate(X_PIECES):
                            if g == g0:
                                pe.wait_ge(x_loaded[piece], 16 * (at[0] + 1))
                        wait(pe, xt_low, number(*at))
                        wait(pe, xt_high, number(*at))
                        for k, c in enumerate(chunks_of(g)):
                            ins = transpose(xt_ps[:, k * P:(k + 1) * P], x[:, c * P:(c + 1) * P])
                        ins.then_inc(xt_full, 1)
                    if (at := group_at(j, slot, 1)) is not None:
                        g, n = at[1], len(chunks_of(at[1])) * P
                        if not scatter and at == (0, 0):
                            pe.wait_ge(setup_sb, 2)
                            pe.wait_ge(first_filled, 4)
                        pe.wait_ge(xt_low, number(*at) + 1)
                        pe.wait_ge(xt_high, number(*at) + 1)
                        if kind_of(g) <= 2:
                            if scatter or at[0] > 0 or g == 6:
                                pe.wait_ge(fill_0, 16 * (8 * at[0] + 4))
                        else:
                            pe.wait_ge(fill_1, 16 * 4 * (at[0] + 1))
                        wait(pe, h_ready, freed(*at))
                        for half in range(2):
                            ins = pe.matmul(a_ps[g % 2][HID * half:HID * (half + 1), 0:n], w_t[:, half, :],
                                            xt[:, kind_of(g), half, 0:n], start=True, stop=True)
                        ins.then_inc(a_full, 1)
                    if j_is(j, -2) and slot == HEAD_SLOT + 2:
                        transpose_last()
                    if chain and slot == SCORES_SLOT + 1:
                        pe.wait_ge(s_ready, s + 1)
                        wait(pe, pt_ready, s)
                        for c in range(4):
                            ins = transpose(misc_ps[:, c * P:(c + 1) * P], s_sb[:, c * P:(c + 1) * P])
                        ins.then_inc(st_full, 1)
                    if chain and slot == softmax_slot(3, scatter):
                        pe.wait_ge(softmax_step, 6 * s + 6)
                        transpose(misc_ps[0:PAIR, 0:P], prob[:, :]).then_inc(pt_full, 1)
                    if scatter:
                        if pool_makes_a(j, slot):
                            pe.wait_ge(a_by_pool, made_by_pool(j, slot + 1))
                            pe.wait_ge(oh_ready, SLOTS * j + slot + 1)
                        else:
                            pe.wait_ge(ab_ready, count_a(j, slot) + 1)
                        for u in range(NU):
                            unit = NU * slot + u
                            pe.wait_ge(out_ready, OUT_BANKS + NU * SLOTS * j + unit_before(unit) + 1)
                            for q in range(UNIT):
                                pair = UNIT * u + q
                                for part in range(PARTS):
                                    ins = pe.matmul(out_ps[unit % OUT_BANKS][0:ROWS, q * RUN:(q + 1) * RUN],
                                                    a_w[slot % AB][:, pair, part, :],
                                                    b_w[slot // 2][:, BATCH_PAIRS * (slot % 2) + pair, :],
                                                    start=part == 0, stop=part == PARTS - 1)
                            ins.then_inc(out_full, 1)

            pe.wait_ge(consts, 2)
            pe.wait_ge(w_twice, 1)
            for k in range(2):
                ins = transpose(misc_ps[:, k * HID:(k + 1) * HID], w_nat[:, k:k + 2, :])
            ins.then_inc(setup_ps, 1)
            pe.wait_ge(last_twice, 1)
            for r in range(2):
                ins = transpose(a_ps[0][:, r * P:(r + 1) * P], last_nat[:, 0, r, :, :])
            ins.then_inc(setup_ps, 1)
            pe.sem_inc(out_full, NU * PLAIN)
            body(-2, scatter=False, slots=range(HEAD_SLOT, SLOTS))
            body(-1, scatter=False)
            pe.wait_ge(codes_sb, SUPERS // 2)
            steps(pe, SUPERS - 2, body, first=1)


ROUND = 1.5 * 2.0 ** 23
ITEM_STEPS = 10


def kernel(**inputs):
    import numpy as np
    import concourse.bacc as bacc
    from concourse.bass_utils import run_bass_kernel_spmd

    nc = bacc.Bacc("TRN2", target_bir_lowering=False, num_devices=1)
    names = ["r_last_memory", "r_all_memory", "r_seq_item", "L0_rec_Wr", "L0_rec_Ur", "L0_rec_Vr_w", "L0_rec_Vr_b"]
    arrays, args = {}, []
    for name in names:
        a = np.ascontiguousarray(inputs[name])
        if a.ndim == 0:
            a = a.reshape(1)
        arrays[name] = a
        args.append(nc.dram_tensor(name, a.shape, mybir.dt.from_np(a.dtype), kind="ExternalInput").ap())
    out = nc.dram_tensor("out", (BATCH, ITEMS), F32, kind="ExternalOutput").ap()
    build(nc, *args, out)
    r = run_bass_kernel_spmd(nc, [arrays], core_ids=[0])
    return r.results[0]["out"]
```
